# Optimizing a Trainium2 kernel written in Bass

```python
import numpy as np
import jax
import jax.numpy as jnp

def _softmax(x, axis=-1):
    return jax.nn.softmax(x, axis=axis)

def _gelu(x):
    return jax.nn.gelu(x, approximate=True)

def _silu(x):
    return jax.nn.silu(x)

def _sigmoid(x):
    return jax.nn.sigmoid(x)

def _layernorm(x, axis=-1, eps=1e-05):
    m = jnp.mean(x, axis=axis, keepdims=True)
    v = jnp.var(x, axis=axis, keepdims=True)
    return (x - m) / jnp.sqrt(v + eps)

def _scatter_add(tgt, idx, src, axis=0):
    return tgt.at[idx].add(src)

def _segment_sum(src, seg, n):
    return jax.ops.segment_sum(src, seg, n)
kernel_name = 'mk_decoder_postln_d1_seqx_r8_706d42'

def setup_inputs(seed: int=0):
    np.random.seed(seed)
    _w = jnp.asarray

    def _rec_inputs():
        import jax
        import jax.numpy as jnp
        _rk = jax.random.key(seed)
        x = 2.818e-05 + 1 * jax.random.normal(jax.random.fold_in(_rk, 1), (4, 256, 256), jnp.float32)
        _lenS = 256 - jax.random.randint(jax.random.fold_in(_rk, 7), (4,), 0, max(1, 256 // 4) + 1, jnp.int32)
        _lenS2 = 256 - jax.random.randint(jax.random.fold_in(_rk, 8), (4,), 0, max(1, 256 // 4) + 1, jnp.int32)
        _ctx_1024P = jax.random.normal(jax.random.fold_in(_rk, 11), (4, 16, 128), jnp.float32)
        _ctx_1024c = jax.random.dirichlet(jax.random.fold_in(_rk, 511), 0.3 * jnp.ones((16,), jnp.float32), (4, 256))
        _ctx_1024t = jnp.einsum('bsk,bkd->bsd', _ctx_1024c, _ctx_1024P)
        _ctx_1024t = _ctx_1024t * jax.lax.rsqrt(jnp.mean(jnp.square(_ctx_1024t)) + 1e-12) * 0.953939
        ctx_1024 = 7.22013e-05 + 1.00017 * (_ctx_1024t + 0.3 * jax.random.normal(jax.random.fold_in(_rk, 611), (4, 256, 128), jnp.float32))
        return (x, ctx_1024)
    x, ctx_1024 = _rec_inputs()

    def _L0_attn_setup():
        import jax, jax.numpy as jnp
        import numpy as np
        HIDDEN = 256
        N_HEADS = 16
        N_KV = 8
        HEAD_DIM = 128
        WINDOW = 128
        EPS = 1e-06

        def rms_norm(x, w):
            var = jnp.mean(x * x, axis=-1, keepdims=True)
            return x * jax.lax.rsqrt(var + EPS) * w
        key = jax.random.key(seed)
        ks = jax.random.split(key, 8)
        B, L = (2, 256)
        s = 0.02
        return {'hidden_states': jax.random.normal(ks[0], (B, L, HIDDEN), jnp.float32), 'Wq': jax.random.normal(ks[1], (N_HEADS * HEAD_DIM, HIDDEN), jnp.float32) * s, 'Wk': jax.random.normal(ks[2], (N_KV * HEAD_DIM, HIDDEN), jnp.float32) * s, 'Wv': jax.random.normal(ks[3], (N_KV * HEAD_DIM, HIDDEN), jnp.float32) * s, 'Wo': jax.random.normal(ks[4], (HIDDEN, N_HEADS * HEAD_DIM), jnp.float32) * s, 'q_norm_w': jnp.ones((HEAD_DIM,), jnp.float32), 'k_norm_w': jnp.ones((HEAD_DIM,), jnp.float32)}
    _L0_attn_all = _L0_attn_setup()
    _L0_attn_in = {k: v for k, v in _L0_attn_all.items() if k in ('Wq', 'Wk', 'Wv', 'Wo', 'q_norm_w', 'k_norm_w')}
    del _L0_attn_all

    def _L0_xattn_setup():
        import jax, jax.numpy as jnp
        import numpy as np
        B_, L_, D_MODEL = (4, 256, 128)
        D_STATE, D_CONV, EXPAND = (16, 4, 2)
        D_INNER = EXPAND * D_MODEL
        DT_RANK = (D_MODEL + 15) // 16

        def silu(x):
            return x * jax.nn.sigmoid(x)
        key = jax.random.key(seed)
        ks = jax.random.split(key, 10)
        f32 = jnp.float32
        hidden_states = jax.random.normal(ks[0], (B_, L_, D_MODEL), dtype=f32)
        z = jax.random.normal(ks[1], (B_, D_INNER, L_), dtype=f32)
        in_proj_w = jax.random.normal(ks[2], (D_INNER, D_MODEL), dtype=f32) * 0.02
        conv_w = jax.random.normal(ks[3], (D_INNER, 1, D_CONV), dtype=f32) * 0.1
        conv_b = jax.random.normal(ks[4], (D_INNER,), dtype=f32) * 0.02
        x_proj_w = jax.random.normal(ks[5], (DT_RANK + 2 * D_STATE, D_INNER), dtype=f32) * 0.02
        dt_proj_w = jax.random.uniform(ks[6], (D_INNER, DT_RANK), dtype=f32, minval=-DT_RANK ** (-0.5), maxval=DT_RANK ** (-0.5))
        dt = jnp.exp(jax.random.uniform(ks[7], (D_INNER,), dtype=f32, minval=np.log(0.001), maxval=np.log(0.1)))
        dt_proj_b = jnp.log(jnp.expm1(dt))
        A_log = jnp.log(jnp.broadcast_to(jnp.arange(1, D_STATE + 1, dtype=f32), (D_INNER, D_STATE)))
        D = jnp.ones((D_INNER,), f32)
        return {'hidden_states': hidden_states, 'z': z, 'in_proj_w': in_proj_w, 'conv_w': conv_w, 'conv_b': conv_b, 'x_proj_w': x_proj_w, 'dt_proj_w': dt_proj_w, 'dt_proj_b': dt_proj_b, 'A_log': A_log, 'D': D}
    _L0_xattn_all = _L0_xattn_setup()
    _L0_xattn_in = {k: v for k, v in _L0_xattn_all.items() if k in ('in_proj_w', 'conv_w', 'conv_b', 'x_proj_w', 'dt_proj_w', 'dt_proj_b', 'A_log', 'D')}
    del _L0_xattn_all

    def _L0_ffn_setup():
        import jax, jax.numpy as jnp
        import numpy as np
        EPS = 1e-05
        NUM_BITS = 8

        def _round_ste(x):
            return x + jax.lax.stop_gradient(jnp.round(x) - x)

        def _clamp_ste(x, lo=-1.0, hi=1.0):
            return x + jax.lax.stop_gradient(jnp.clip(x, lo, hi) - x)

        def ternary_quantize(w):
            scale = jnp.maximum(jnp.mean(jnp.abs(w)), EPS)
            q = _clamp_ste(_round_ste(w / scale))
            return scale * q

        def quantized_relu2(x, num_bits=NUM_BITS, eps=EPS):
            x = jnp.square(jax.nn.relu(x))
            xmax = jnp.maximum(jnp.max(x, axis=-1, keepdims=True), eps)
            num_steps = 2 ** num_bits - 1
            return _round_ste(x / xmax * num_steps) / num_steps * xmax
        key = jax.random.key(seed)
        k1, k2, k3 = jax.random.split(key, 3)
        B, S, D = (4, 256, 256)
        H = 4 * D
        std = 0.5 * D ** (-0.5)
        x = jax.random.normal(k1, (B, S, D), dtype=jnp.float32)
        c_fc = jax.random.normal(k2, (D, H), dtype=jnp.float32) * std
        c_proj = jax.random.normal(k3, (D, H), dtype=jnp.float32) * std
        return {'x': x, 'c_fc': c_fc, 'c_proj': c_proj}
    _L0_ffn_all = _L0_ffn_setup()
    _L0_ffn_in = {k: v for k, v in _L0_ffn_all.items() if k in ('c_fc', 'c_proj')}
    del _L0_ffn_all
    return {'x': x, 'ctx_1024': ctx_1024, 'L0_attn_Wq': _L0_attn_in['Wq'], 'L0_attn_Wk': _L0_attn_in['Wk'], 'L0_attn_Wv': _L0_attn_in['Wv'], 'L0_attn_Wo': _L0_attn_in['Wo'], 'L0_attn_q_norm_w': _L0_attn_in['q_norm_w'], 'L0_attn_k_norm_w': _L0_attn_in['k_norm_w'], 'L0_xattn_in_proj_w': _L0_xattn_in['in_proj_w'], 'L0_xattn_conv_w': _L0_xattn_in['conv_w'], 'L0_xattn_conv_b': _L0_xattn_in['conv_b'], 'L0_xattn_x_proj_w': _L0_xattn_in['x_proj_w'], 'L0_xattn_dt_proj_w': _L0_xattn_in['dt_proj_w'], 'L0_xattn_dt_proj_b': _L0_xattn_in['dt_proj_b'], 'L0_xattn_A_log': _L0_xattn_in['A_log'], 'L0_xattn_D': _L0_xattn_in['D'], 'L0_ffn_c_fc': _L0_ffn_in['c_fc'], 'L0_ffn_c_proj': _L0_ffn_in['c_proj']}

def reference(x, ctx_1024, L0_attn_Wq, L0_attn_Wk, L0_attn_Wv, L0_attn_Wo, L0_attn_q_norm_w, L0_attn_k_norm_w, L0_xattn_in_proj_w, L0_xattn_conv_w, L0_xattn_conv_b, L0_xattn_x_proj_w, L0_xattn_dt_proj_w, L0_xattn_dt_proj_b, L0_xattn_A_log, L0_xattn_D, L0_ffn_c_fc, L0_ffn_c_proj):
    import jax
    import jax.numpy as jnp

    def _L0_attn_ref(hidden_states, Wq, Wk, Wv, Wo, q_norm_w, k_norm_w):
        import jax, jax.numpy as jnp
        import numpy as np
        HIDDEN = 256
        N_HEADS = 16
        N_KV = 8
        HEAD_DIM = 128
        WINDOW = 128
        EPS = 1e-06

        def rms_norm(x, w):
            var = jnp.mean(x * x, axis=-1, keepdims=True)
            return x * jax.lax.rsqrt(var + EPS) * w
        B, L, H = hidden_states.shape
        scale = HEAD_DIM ** (-0.5)
        n_rep = N_HEADS // N_KV
        q = (hidden_states @ Wq.T).reshape(B, L, N_HEADS, HEAD_DIM)
        k = (hidden_states @ Wk.T).reshape(B, L, N_KV, HEAD_DIM)
        v = (hidden_states @ Wv.T).reshape(B, L, N_KV, HEAD_DIM)
        q = rms_norm(q, q_norm_w)
        k = rms_norm(k, k_norm_w)
        q = q.transpose(0, 2, 1, 3)
        k = k.transpose(0, 2, 1, 3)
        v = v.transpose(0, 2, 1, 3)
        k = jnp.repeat(k, n_rep, axis=1)
        v = jnp.repeat(v, n_rep, axis=1)
        scores = jnp.einsum('bhqd,bhkd->bhqk', q, k) * scale
        row = jnp.arange(L)[:, None]
        col = jnp.arange(L)[None, :]
        if L > WINDOW:
            mask = (col >= L - WINDOW) & (col <= row)
        else:
            mask = col > row
        scores = jnp.where(mask[None, None], -jnp.inf, scores)
        probs = jax.nn.softmax(scores, axis=-1)
        out = jnp.einsum('bhqk,bhkd->bhqd', probs, v)
        out = out.transpose(0, 2, 1, 3).reshape(B, L, N_HEADS * HEAD_DIM)
        return out @ Wo.T

    def _L0_xattn_ref(hidden_states, z, in_proj_w, conv_w, conv_b, x_proj_w, dt_proj_w, dt_proj_b, A_log, D):
        import jax, jax.numpy as jnp
        import numpy as np
        B_, L_, D_MODEL = (4, 256, 128)
        D_STATE, D_CONV, EXPAND = (16, 4, 2)
        D_INNER = EXPAND * D_MODEL
        DT_RANK = (D_MODEL + 15) // 16

        def silu(x):
            return x * jax.nn.sigmoid(x)
        Bsz, L, _ = hidden_states.shape
        d_inner, _, d_conv = conv_w.shape
        dt_rank = dt_proj_w.shape[1]
        d_state = A_log.shape[1]
        x = jnp.einsum('bld,ed->bel', hidden_states, in_proj_w)
        xc = jax.lax.conv_general_dilated(x, conv_w, window_strides=(1,), padding=[(d_conv - 1, 0)], feature_group_count=d_inner, dimension_numbers=('NCH', 'OIH', 'NCH'))
        x = silu(xc + conv_b[None, :, None])
        x_dbl = jnp.einsum('bdl,ed->bel', x, x_proj_w)
        dt_low, Bm, Cm = jnp.split(x_dbl, [dt_rank, dt_rank + d_state], axis=1)
        dt = jnp.einsum('brl,dr->bdl', dt_low, dt_proj_w)
        dt = jax.nn.softplus(dt + dt_proj_b[None, :, None])
        A = -jnp.exp(A_log)
        dt_t = jnp.moveaxis(dt, -1, 0)
        B_t = jnp.moveaxis(Bm, -1, 0)
        C_t = jnp.moveaxis(Cm, -1, 0)
        u_t = jnp.moveaxis(x, -1, 0)

        def step(state, inp):
            d, b, c, u = inp
            dA = jnp.exp(d[..., None] * A)
            state = state * dA + (d * u)[..., None] * b[:, None, :]
            y = jnp.einsum('bdn,bn->bd', state, c)
            return (state, y)
        state0 = jnp.zeros((Bsz, d_inner, d_state), x.dtype)
        _, ys = jax.lax.scan(step, state0, (dt_t, B_t, C_t, u_t))
        y = jnp.moveaxis(ys, 0, 2)
        y = y + D[None, :, None] * x
        y = y * silu(z)
        return jnp.swapaxes(y, 1, 2)

    def _L0_ffn_ref(x, c_fc, c_proj):
        import jax, jax.numpy as jnp
        import numpy as np
        EPS = 1e-05
        NUM_BITS = 8

        def _round_ste(x):
            return x + jax.lax.stop_gradient(jnp.round(x) - x)

        def _clamp_ste(x, lo=-1.0, hi=1.0):
            return x + jax.lax.stop_gradient(jnp.clip(x, lo, hi) - x)

        def ternary_quantize(w):
            scale = jnp.maximum(jnp.mean(jnp.abs(w)), EPS)
            q = _clamp_ste(_round_ste(w / scale))
            return scale * q

        def quantized_relu2(x, num_bits=NUM_BITS, eps=EPS):
            x = jnp.square(jax.nn.relu(x))
            xmax = jnp.maximum(jnp.max(x, axis=-1, keepdims=True), eps)
            num_steps = 2 ** num_bits - 1
            return _round_ste(x / xmax * num_steps) / num_steps * xmax
        w1 = ternary_quantize(c_fc)
        h = jnp.einsum('bsd,dh->bsh', x, w1)
        h = quantized_relu2(h, num_bits=NUM_BITS)
        w2 = ternary_quantize(c_proj)
        out = jnp.einsum('bsh,dh->bsd', h, w2)
        return out
    x = _layernorm(x + _L0_attn_ref(x, L0_attn_Wq, L0_attn_Wk, L0_attn_Wv, L0_attn_Wo, L0_attn_q_norm_w, L0_attn_k_norm_w), axis=-1)
    x = _layernorm(x + _L0_xattn_ref(ctx_1024, x, L0_xattn_in_proj_w, L0_xattn_conv_w, L0_xattn_conv_b, L0_xattn_x_proj_w, L0_xattn_dt_proj_w, L0_xattn_dt_proj_b, L0_xattn_A_log, L0_xattn_D), axis=-1)
    x = _layernorm(x + _L0_ffn_ref(x, L0_ffn_c_fc, L0_ffn_c_proj), axis=-1)
    return x

_drawn_inputs = setup_inputs


def setup_inputs(seed=0):
    import zlib

    import numpy as np

    out = dict(_drawn_inputs(seed))
    spreads = {'L0_attn_q_norm_w': (1.0, 0.6), 'L0_attn_k_norm_w': (1.0, 0.6), 'L0_xattn_D': (1.0, 0.6)}
    factors = {'ctx_1024': 4.279,
     'L0_xattn_in_proj_w': 4.296,
     'L0_xattn_conv_w': 4.488,
     'L0_xattn_conv_b': 8.0,
     'L0_xattn_x_proj_w': 8.0,
     'L0_xattn_dt_proj_w': 8.0,
     'L0_xattn_dt_proj_b': 8.0,
     'L0_xattn_A_log': 8.0}
    for name, (base, spread) in spreads.items():
        noise = np.random.default_rng([zlib.crc32(name.encode()), seed]).standard_normal(out[name].shape)
        drawn = base * np.exp(spread * noise) if base else spread * noise
        out[name] = jnp.asarray(drawn.astype(out[name].dtype))
    for name, factor in factors.items():
        out[name] = (out[name] * factor).astype(out[name].dtype)
    return out
```

```python
import concourse.bass as bass
from concourse import mybir
from contextlib import ExitStack

B, L, HID = 4, 256, 256
T = B * L
P = 128
HEADS, KV_HEADS, HD = 16, 8, 128
REP = HEADS // KV_HEADS
WINDOW = 128
CTX = 128
DI, NS, RANK, TAPS = 256, 16, 8, 4
FF = 1024
LT = L // P
HC = HID // P
DC = DI // P
FC = FF // P
GW = (REP + 2) * HD
STEPS = KV_HEADS * B
BC = 2 * NS
RMS_EPS, LN_EPS, Q_EPS = 1e-6, 1e-5, 1e-5
SCALE = float(HD) ** -0.5
LEVELS = 255.0
ROUND = 1.5 * 2.0 ** 23
MASKED = -1e30


def decoder_layer(nc, x, xT, ctxT, w_qkvT, w_oT, q_norm, k_norm, in_projT, conv_wT, conv_b, x_projT,
                  dt_projT, dt_b, a_log, d_skip, c_fc, c_projT, out):
    f32, bf16 = mybir.dt.float32, mybir.dt.bfloat16
    ALU = mybir.AluOpType
    ACT = mybir.ActivationFunctionType
    AX = mybir.AxisListType

    ctx = ExitStack()
    with ctx:
        def sb(name, shape, dt=f32):
            return ctx.enter_context(nc.sbuf_tensor(name, shape, dt))

        def sem(name):
            return ctx.enter_context(nc.semaphore(name))

        xT_sb = sb("xT_sb", [P, HC, T])
        w_sb = sb("w_sb", [P, KV_HEADS, HC, GW])
        attnT = sb("attnT", [P, HEADS, T])
        u = sb("u", [P, DC, T])
        dt = sb("dt", [P, DC, T])
        du = sb("du", [P, DC, T])
        y = sb("y", [P, DC, T])
        work = sb("work", [P, 10 * T])

        w_flat = w_sb[:, :, :, :].rearrange("p g c n -> p (g c n)")
        wo_sb = w_flat[:, 0:HEADS * HID].rearrange("p (h n) -> p h n", h=HEADS)
        fc_sb = w_flat[:, 4096:6144].rearrange("p (c n) -> p c n", c=HC)
        pr_sb = w_flat[:, 6144:8192].rearrange("p (c n) -> p c n", c=FC)
        x_sb = u[:, :, :].rearrange("p c t -> p (c t)").rearrange("p (i n) -> p i n", n=HID)
        early = attnT[:, HEADS // 2:, :].rearrange("p h t -> p (h t)")
        ctxp = early[:, 0:B * (TAPS - 1 + L)].rearrange("p (b l) -> p b l", b=B)
        in_sb = early[:, 1280:1280 + DI]
        cw_sb = early[:, 2048:2048 + TAPS * DI].rearrange("p (k e) -> p k e", k=TAPS)
        win = early[:, 3072:3072 + TAPS * DI].rearrange("p (k e) -> p k e", k=TAPS)
        xdbl = early[0:BC + RANK, 4096:4096 + T]
        dtw_sb = early[0:BC + RANK, 5120:5120 + DI]
        xp_sb = early[:, 6144:6144 + DC * (BC + RANK)].rearrange("p (c n) -> p c n", c=DC)
        absv = early[:, 6400:6400 + DC * L].rearrange("p (c l) -> p c l", c=DC)
        lost = early[:, 6912:6912 + DC * L].rearrange("p (c l) -> p c l", c=DC)
        ln_out = early[:, 2048:2048 + DC * T].rearrange("p (c t) -> p c t", c=DC)
        bc = work[:, 0:4 * T].rearrange("p (s k t) -> p s k t", s=2, k=2)
        dA = work[:, 4 * T:6 * T].rearrange("p (s b l) -> p s b l", s=2, b=B)
        dBu = work[:, 6 * T:7 * T]
        st = work[:, 7 * T:8 * T]
        prod = work[:, 8 * T:10 * T].rearrange("p (s t) -> p s t", s=2)
        cb_sb = sb("cb_sb", [P, DC])
        dtb_sb = sb("dtb_sb", [P, DC])
        alog_sb = sb("alog_sb", [P, DC, NS])
        d_sb = sb("d_sb", [P, DC])
        qn_sb = sb("qn_sb", [P, 1])
        kn_sb = sb("kn_sb", [P, 1])
        ident = sb("ident", [P, P])
        ident16 = sb("ident16", [P, P], bf16)
        mask16 = sb("mask16", [P, P], bf16)
        eps_rms = sb("eps_rms", [P, 1])
        eps_ln = sb("eps_ln", [P, 1])
        ncb = sb("ncb", [P, DC])
        A = sb("A", [P, DC, NS])
        expA = sb("expA", [P, DC, NS])
        qk_raw = sb("qk_raw", [P, LT, (REP + 1) * HD])
        square = sb("square", [P, LT, REP + 1, HD], bf16)
        ssq = sb("ssq", [P, 2, LT * (REP + 1)])
        lnr = sb("lnr", [P, 2, LT * (REP + 1)])
        rinv = sb("rinv", [P, 2, LT * (REP + 1)])
        wqk = sb("wqk", [P, 1])
        v_sb = sb("v_sb", [P, 4, LT, HD])
        qT = sb("qT", [P, REP * L])
        kT = sb("kT", [P, L])
        mx = sb("mx", [P, LT * REP])
        nbias = sb("nbias", [P, 2, LT * REP])
        rowsum = sb("rowsum", [P, 2, LT * REP])
        rsinv = sb("rsinv", [P, 2, LT * REP])
        probs = sb("probs", [P, 2, LT, REP, L])
        pT = sb("pT", [P, LT, REP * L])
        def tiles(region):
            return region.rearrange("p (t n) -> p t n", t=LT)

        probs_flat = probs[:, 0].rearrange("p t j l -> p (t j l)")
        pT_flat = pT[:, :, :].rearrange("p t l -> p (t l)")
        oT, x1p = tiles(probs_flat[:, 0:512]), tiles(probs_flat[:, 512:1024])
        gated, x2p = tiles(pT_flat[:, 0:512]), tiles(pT_flat[:, 512:1024])
        x1 = tiles(qk_raw[:, :, :].rearrange("p t n -> p (t n)")[:, 0:512])
        ex = tiles(v_sb[:, 0:2].rearrange("p s t n -> p (s t n)"))
        x2, r1, x2_kept, x3p, x3 = (tiles(work[:, 512 * k:512 * (k + 1)]) for k in range(5))
        act_sq = tiles(work[:, 5120:7168])
        act_q = tiles(work[:, 7168:8192].bitcast(bf16))
        act_qT = work[:, 8192:9216].bitcast(bf16).rearrange("p (t c n) -> p t c n", t=LT, c=FC)
        parts = work[:, 9216:9984].bitcast(bf16).rearrange("p (i c n) -> p i c n", i=3, c=HC)
        w1q = xT_sb[:, 0, :].bitcast(bf16).rearrange("p (c n) -> p c n", c=HC)
        w2q = xT_sb[:, 1, :].bitcast(bf16).rearrange("p (c n) -> p c n", c=FC)
        stats = sb("stats", [P, 3, LT, 6])
        mv = sb("mv", [P, 3, LT, 2])
        lnv = sb("lnv", [P, 3, LT])
        rstd = sb("rstd", [P, 3, LT])
        asum = sb("asum", [P, 2])
        atot = sb("atot", [P, 2])
        wscale = sb("wscale", [P, 2])
        winv = sb("winv", [P, 2])
        up_c = sb("up_c", [P, 1])
        down_c = sb("down_c", [P, 1])
        hmax = sb("hmax", [P, LT])
        hs = sb("hs", [P, LT])
        hs2 = sb("hs2", [P, LT])
        xmax = sb("xmax", [P, LT])
        xinv = sb("xinv", [P, LT])
        q_mul = sb("q_mul", [P, LT])
        o_mul = sb("o_mul", [P, LT])

        PA = ctx.enter_context(nc.psum_tensor("PA", [P, 2, 512], f32))
        PB = ctx.enter_context(nc.psum_tensor("PB", [P, 2, 512], f32))
        PC = ctx.enter_context(nc.psum_tensor("PC", [P, 2, 512], f32))
        PD = ctx.enter_context(nc.psum_tensor("PD", [P, 2, 512], f32))

        bc_dram = nc.dram_tensor("bc_scratch", [NS, 2, T], f32, kind="Internal").ap()

        ctx_in = sem("ctx_in")
        ssm_in = sem("ssm_in")
        small_in = sem("small_in")
        xT_in = sem("xT_in")
        w_in = [sem("w0_in"), sem("w1_in")]
        w_rest = sem("w_rest")
        wo_in = sem("wo_in")
        fc_in = sem("fc_in")
        pr_in = sem("pr_in")
        x_in = sem("x_in")
        zeroed = sem("zeroed")
        const_ready = sem("const_ready")
        win_ready = sem("win_ready")
        ncb_ready = sem("ncb_ready")
        conv_done = sem("conv_done")
        expv_ready = sem("expv_ready")
        den_ready = sem("den_ready")
        sig_ready = sem("sig_ready")
        u_ready = sem("u_ready")
        xdbl_done = sem("xdbl_done")
        xdbl_ready = sem("xdbl_ready")
        dt_done = sem("dt_done")
        sp_abs = sem("sp_abs")
        sp_relu = sem("sp_relu")
        sp_exp = sem("sp_exp")
        sp_w1 = sem("sp_w1")
        sp_lost = sem("sp_lost")
        sp_rest = sem("sp_rest")
        bc_stored = sem("bc_stored")
        sp_ln = sem("sp_ln")
        sp_gate = sem("sp_gate")
        dt_ready = sem("dt_ready")
        du_ready = sem("du_ready")
        expA_ready = sem("expA_ready")
        A_ready = sem("A_ready")
        bc_loaded = [sem("bc_even"), sem("bc_odd")]
        dA_free = sem("dA_free")
        dA_ready = sem("dA_ready")
        dBu_ready = sem("dBu_ready")
        prod_ready = sem("prod_ready")
        y_added = sem("y_added")
        proj_done = sem("proj_done")
        ssq_ready = sem("ssq_ready")
        ln_ready = sem("ln_ready")
        rinv_ready = sem("rinv_ready")
        v_ready = sem("v_ready")
        qk_raw_ready = sem("qk_raw_ready")
        k_norm_ready = sem("k_norm_ready")
        wqk_ready = sem("wqk_ready")
        qkT_done = sem("qkT_done")
        qT_ready = sem("qT_ready")
        kT_ready = sem("kT_ready")
        scores_done = sem("scores_done")
        mx_ready = sem("mx_ready")
        nbias_ready = sem("nbias_ready")
        exp_done = sem("exp_done")
        rsinv_ready = sem("rsinv_ready")
        norm_begun = sem("norm_begun")
        normed = sem("normed")
        pT_done = sem("pT_done")
        pT_half0 = sem("pT_half0")
        pT_half1 = sem("pT_half1")
        pv_done = sem("pv_done")
        attn_ready = sem("attn_ready")

        eps_ready = sem("eps_ready")
        abs_ready = sem("abs_ready")
        abs_summed = sem("abs_summed")
        wscale_ready = sem("wscale_ready")
        winv_ready = sem("winv_ready")
        up_ready = sem("up_ready")
        w_scaled = sem("w_scaled")
        w_clipped = sem("w_clipped")
        ternary_ready = sem("ternary_ready")
        wo_done = sem("wo_done")
        oT_ready = sem("oT_ready")
        back_done = sem("back_done")
        xp_ready = [sem(f"x{k + 1}p_ready") for k in range(3)]
        stats_ready = [sem(f"stats{k + 1}_ready") for k in range(3)]
        mv_ready = [sem(f"mv{k + 1}_ready") for k in range(3)]
        lnv_ready = [sem(f"lnv{k + 1}_ready") for k in range(3)]
        rstd_ready = [sem(f"rstd{k + 1}_ready") for k in range(3)]
        xn_ready = [sem(f"x{k + 1}_ready") for k in range(3)]
        ez_ready = sem("ez_ready")
        ez1_ready = sem("ez1_ready")
        sz_ready = sem("sz_ready")
        z_ready = sem("z_ready")
        gated_ready = sem("gated_ready")
        gT_done = sem("gT_done")
        x2T_done = sem("x2T_done")
        part1_ready = sem("part1_ready")
        rest1_ready = sem("rest1_ready")
        part2_ready = sem("part2_ready")
        part3_ready = sem("part3_ready")
        up_done = sem("up_done")
        relu_ready = sem("relu_ready")
        sq_ready = sem("sq_ready")
        hs_ready = sem("hs_ready")
        hs2_ready = sem("hs2_ready")
        xmax_ready = sem("xmax_ready")
        xinv_ready = sem("xinv_ready")
        mul_ready = sem("mul_ready")
        rounded = sem("rounded")
        act_q_ready = sem("act_q_ready")
        act_T_done = sem("act_T_done")
        act_qT_ready = sem("act_qT_ready")
        down_done = sem("down_done")
        kept = sem("kept")
        stored = sem("stored")

        def reach(eng, s, value):
            if not (isinstance(value, int) and value <= 0):
                eng.wait_ge(s, value)

        def fixed(g):
            return isinstance(g, int)

        def groups(eng, body):
            body(0)
            with eng.Fori(1, KV_HEADS - 1) as g:
                body(g)
            body(KV_HEADS - 1)

        def batches(eng, body):
            body(0)
            with eng.Fori(1, B - 1) as i:
                body(i)
            body(B - 1)
            body(B)

        def begins(i):
            return not fixed(i) or i < B

        def ends(i):
            return not fixed(i) or i > 0

        def follows(i):
            return not fixed(i) or i + 1 < B

        def has_step(g, b, ahead):
            return not fixed(g) or 0 <= B * g + b + ahead < STEPS

        block = ctx.enter_context(nc.Block())

        @block.sync
        def _(sp):
            sp.dma_start(w_sb[:, 0], w_qkvT[0].rearrange("(c p) n -> p c n", p=P)).then_inc(w_in[0], 16)
            sp.dma_start(in_sb, in_projT).then_inc(ssm_in, 16)
            sp.dma_start(cw_sb, conv_wT.partition_broadcast(P)).then_inc(ssm_in, 16)
            sp.dma_start(ctxp[:, :, TAPS - 1:], ctxT.rearrange("c (b l) -> c b l", b=B)).then_inc(ctx_in, 16)
            sp.dma_start(w_sb[:, 1], w_qkvT[1].rearrange("(c p) n -> p c n", p=P)).then_inc(w_in[1], 16)

            def load_weights(g):
                sp.dma_start(w_sb[:, bass.ds(g, 1)].rearrange("p o c n -> p (o c) n"),
                             w_qkvT[bass.ds(g, 1)].rearrange("o (c p) n -> p (o c) n", p=P)).then_inc(w_rest, 16)

            load_weights(2)
            with sp.Fori(3, KV_HEADS) as g:
                sp.wait_ge(w_rest, g * 16 - 32)
                load_weights(g)

            sp.wait_ge(xdbl_ready, B)
            sp.dma_start(bc_dram.rearrange("n k t -> (n k) t"), xdbl[0:BC, :]).then_inc(bc_stored, 16)
            sp.wait_ge(bc_stored, 16)

            def load_bc(n):
                for k in range(2):
                    reach(sp, prod_ready, B * n - B + 2 * k + 2 if not (fixed(n) and n == 0) else 0)
                    sp.dma_start(bc[:, k], bc_dram[bass.ds(n * 2 + k, 1)].rearrange("o k t -> (o k) t")
                                 .partition_broadcast(P)).then_inc(bc_loaded[k], 16)

            load_bc(0)
            sp.wait_ge(y_added, DC)
            sp.wait_ge(du_ready, DC)
            sp.dma_start(x_sb, x.rearrange("(i p) n -> p i n", p=P)).then_inc(x_in, 16)
            with sp.Fori(1, KV_HEADS - 2) as n:
                load_bc(n)
            sp.wait_ge(proj_done, 6 * B * LT)
            sp.dma_start(fc_sb, c_fc.rearrange("(c p) n -> p c n", p=P)).then_inc(fc_in, 16)
            sp.dma_start(wo_sb, w_oT.rearrange("(h p) n -> p h n", p=P)).then_inc(wo_in, 16)
            load_bc(KV_HEADS - 2)
            sp.wait_ge(proj_done, 8 * B * LT)
            sp.dma_start(pr_sb, c_projT.rearrange("(c p) n -> p c n", p=P)).then_inc(pr_in, 16)
            load_bc(KV_HEADS - 1)

            def store(b):
                sp.wait_ge(xn_ready[2], b + 1)
                sp.dma_start(out[bass.ds(b * L, L)].rearrange("(t p) n -> p t n", p=P), x3).then_inc(stored, 16)

            with sp.Fori(0, B) as b:
                store(b)
            sp.wait_ge(stored, 16 * B)

        @block.gpsimd
        def _(pool):
            nc.gpsimd.memset(ctxp[:, :, 0:TAPS - 1], 0.0).then_inc(zeroed, 1)
            nc.gpsimd.memset(ident[:, :], 0.0).then_inc(zeroed, 1)
            nc.gpsimd.memset(ident16[:, :], 0.0).then_inc(zeroed, 1)
            nc.gpsimd.memset(mask16[:, :], 0.0).then_inc(zeroed, 1)
            for k in range(2):
                nc.gpsimd.memset(dA[:, k, :, 0:1], 0.0).then_inc(dA_free, 1)
            pool.wait_ge(zeroed, 4)
            for m in (ident, ident16):
                nc.gpsimd.affine_select(out=m[:, :], in_=m[:, :], compare_op=ALU.not_equal, fill=1.0, base=0,
                                        pattern=[[-1, P]], channel_multiplier=1).then_inc(const_ready, 1)
            nc.gpsimd.affine_select(out=mask16[:, :], in_=mask16[:, :], compare_op=ALU.is_gt, fill=MASKED, base=0,
                                    pattern=[[1, P]], channel_multiplier=-1).then_inc(const_ready, 1)
            pool.wait_ge(small_in, 16 * 6)

            def begin_y():
                for i in range(DC):
                    pool.wait_ge(dt_ready, i + 1)
                    pool.wait_ge(u_ready, B)
                    nc.gpsimd.tensor_tensor(du[:, i], dt[:, i], u[:, i], ALU.mult).then_inc(du_ready, 1)
                    nc.gpsimd.tensor_scalar(y[:, i], u[:, i], d_sb[:, i:i + 1], 1.0, ALU.mult, ALU.mult)\
                        .then_inc(y_added, 1)

            def add_y(k, b):
                pool.wait_ge(prod_ready, k + 1)
                pool.wait_ge(y_added, k + 1)
                nc.gpsimd.tensor_tensor(y[:, b % 2], y[:, b % 2], prod[:, b % 2], ALU.add).then_inc(y_added, 1)

            def sum_abs(k):
                pool.wait_ge(abs_ready, k + 1)
                nc.gpsimd.partition_all_reduce(atot[:, k:k + 1], asum[:, k:k + 1], P, bass.bass_isa.ReduceOp.add)\
                    .then_inc(abs_summed, 1)

            def body(g):
                for b in range(B):
                    s = g * B + b
                    pool.wait_ge(rsinv_ready, s + 1)
                    pool.sem_inc(norm_begun, 1)
                    for t in range(LT):
                        for j in range(REP):
                            last = nc.gpsimd.tensor_scalar(probs[:, b % 2, t, j], probs[:, b % 2, t, j],
                                                           rsinv[:, b % 2, t * REP + j:t * REP + j + 1], 1.0,
                                                           ALU.mult, ALU.mult)
                    last.then_inc(normed, 1)
                    if not (fixed(g) and g == 0):
                        add_y(s - B, b)
                    if fixed(g) and g == KV_HEADS - 1 and b == 0:
                        sum_abs(0)
                if fixed(g) and g == 0:
                    begin_y()

            groups(pool, body)
            for b in range(B):
                add_y(STEPS - B + b, b)
            sum_abs(1)

        @block.scalar
        def _(act):
            act.dma_start(xT_sb[:, :, :], xT.rearrange("(c p) t -> p c t", p=P)).then_inc(xT_in, 16)
            act.dma_start(qn_sb[:, :], q_norm).then_inc(xT_in, 16)
            act.dma_start(kn_sb[:, :], k_norm).then_inc(xT_in, 16)
            for dst, src in ((cb_sb[:, :], conv_b), (xp_sb, x_projT.rearrange("(c p) n -> p c n", p=P)),
                             (dtw_sb[BC:, :], dt_projT), (dtb_sb[:, :], dt_b),
                             (alog_sb[:, :, :], a_log.rearrange("(c p) n -> p c n", p=P)), (d_sb[:, :], d_skip)):
                act.dma_start(dst, src).then_inc(small_in, 16)

            nc.scalar.preload_act_table_set("natural_log_exp_and_others")
            act.wait_ge(small_in, 16 * 6)
            nc.scalar.activation(expA[:, :, :], alog_sb[:, :, :], ACT.Exp).then_inc(expA_ready, 1)
            act.wait_ge(eps_ready, 2)

            def norm(s, b):
                for t in range(LT):
                    act.wait_ge(proj_done, s * LT + t + 1)
                    for j in range(REP + 1):
                        last = nc.scalar.activation(square[:, t, j], PA[:, t, j * HD:(j + 1) * HD], ACT.Square,
                                                    accum_out=ssq[:, b % 2, t * (REP + 1) + j:t * (REP + 1) + j + 1])
                last.then_inc(ssq_ready, 1)
                nc.scalar.activation(qk_raw[:, :, :], PA[:, :, 0:(REP + 1) * HD], ACT.Copy).then_inc(qk_raw_ready, 1)
                act.wait_ge(ssq_ready, s + 1)
                nc.scalar.activation(lnr[:, b % 2], ssq[:, b % 2], ACT.Ln, scale=1.0 / HD, bias=eps_rms[:, :])\
                    .then_inc(ln_ready, 1)
                nc.scalar.activation(v_sb[:, b % 4], PA[:, :, (REP + 1) * HD:], ACT.Copy).then_inc(v_ready, 1)
                act.wait_ge(ln_ready, s + 1)
                nc.scalar.activation(rinv[:, b % 2], lnr[:, b % 2], ACT.Exp, scale=-0.5).then_inc(rinv_ready, 1)

            def take_qT(s):
                act.wait_ge(qkT_done, s + 1)
                nc.scalar.activation(qT[:, :], PB[:, 0, :], ACT.Copy).then_inc(qT_ready, 1)

            def take_pT(s):
                act.wait_ge(pT_done, s + 1)
                nc.scalar.activation(pT[:, 0], PD[:, 0, :], ACT.Copy).then_inc(pT_half0, 1)

            def decay(k, n, b):
                act.wait_ge(dA_free, k + 1)
                nc.scalar.activation(dA[:, b % 2, :, 1:], dt[:, b % 2].rearrange("p (b l) -> p b l", b=B)[:, :, 1:],
                                     ACT.Exp, scale=A[:, b % 2, bass.ds(n, 1)]).then_inc(dA_ready, 1)

            def silu_exp(b):
                act.wait_ge(ncb_ready, 1)
                act.wait_ge(conv_done, b + 1)
                for i in range(DC):
                    nc.scalar.activation(dt[:, i, b * L:(b + 1) * L], PA[:, 1, i * L:(i + 1) * L], ACT.Exp,
                                         bias=ncb[:, i:i + 1], scale=-1.0).then_inc(expv_ready, 1)

            def softplus_exp(b):
                act.wait_ge(dt_done, b + 1)
                for i in range(DC):
                    v = PA[:, 1, i * L:(i + 1) * L]
                    nc.scalar.activation(absv[:, i], v, ACT.Abs, bias=dtb_sb[:, i:i + 1]).then_inc(sp_abs, 1)
                    nc.scalar.activation(dt[:, i, b * L:(b + 1) * L], v, ACT.Relu, bias=dtb_sb[:, i:i + 1])\
                        .then_inc(sp_relu, 1)
                act.wait_ge(sp_abs, (b + 1) * DC)
                nc.scalar.activation(du[:, :, b * L:(b + 1) * L], absv, ACT.Exp, scale=-1.0).then_inc(sp_exp, 1)

            norm(0, 0)
            take_qT(0)

            def body(g):
                for b in range(B):
                    s = g * B + b
                    first = fixed(g) and g == 0
                    if has_step(g, b, 1):
                        norm(s + 1, b + 1)
                    if first:
                        silu_exp(b)
                    if has_step(g, b, -1):
                        take_pT(s - 1)
                    if has_step(g, b, 1):
                        take_qT(s + 1)
                    act.wait_ge(nbias_ready, s + 1)
                    for t in range(LT):
                        for j in range(REP):
                            k = t * REP + j
                            r = t * (REP + 1) + j
                            last = nc.scalar.activation(probs[:, b % 2, t, j], PC[:, t, j * L:(j + 1) * L], ACT.Exp,
                                                        bias=nbias[:, b % 2, k:k + 1], scale=rinv[:, b % 2, r:r + 1],
                                                        accum_out=rowsum[:, b % 2, k:k + 1])
                    last.then_inc(exp_done, 1)
                    if first:
                        softplus_exp(b)
                    else:
                        decay(s - B, g * 2 - 2 + b // 2, b)
                if first:
                    nc.scalar.preload_act_table_set("natural_log")
                    act.wait_ge(sp_exp, B)
                    for i in range(DC):
                        nc.scalar.activation(ln_out[:, i], du[:, i], ACT.Ln, bias=1.0).then_inc(sp_ln, 1)
                    nc.scalar.preload_act_table_set("natural_log_exp_and_others")
                    act.wait_ge(A_ready, 1)
                    act.wait_ge(dt_ready, DC)

            groups(act, body)

            def take_oT(b):
                act.wait_ge(wo_done, b + 1)
                nc.scalar.activation(oT.rearrange("p c n -> p (c n)"), PA[:, 0, :], ACT.Copy).then_inc(oT_ready, 1)

            def rstd_of(k, b):
                act.wait_ge(mv_ready[k], b + 1)
                nc.scalar.activation(lnv[:, k], mv[:, k, :, 1], ACT.Ln, bias=eps_ln[:, :]).then_inc(lnv_ready[k], 1)
                act.wait_ge(lnv_ready[k], b + 1)
                nc.scalar.activation(rstd[:, k], lnv[:, k], ACT.Exp, scale=-0.5).then_inc(rstd_ready[k], 1)

            take_oT(0)

            def tail(i):
                if begins(i):
                    rstd_of(0, i)
                    act.wait_ge(xn_ready[0], i + 1)
                    nc.scalar.activation(ex, x1, ACT.Exp, scale=-1.0).then_inc(ez_ready, 1)
                if fixed(i) and i == 0:
                    take_pT(STEPS - 1)
                    for b in range(B):
                        decay(STEPS - B + b, NS - 2 + b // 2, b)
                if ends(i):
                    for t in range(LT):
                        act.wait_ge(relu_ready, i * LT - LT + t + 1)
                        nc.scalar.activation(act_sq[:, t], act_sq[:, t], ACT.Square).then_inc(sq_ready, 1)
                if begins(i):
                    rstd_of(1, i)
                    act.wait_ge(x2T_done, i + 1)
                    nc.scalar.activation(parts[:, 0], PB[:, 1, :].rearrange("p (c n) -> p c n", c=HC), ACT.Copy)\
                        .then_inc(part1_ready, 1)
                    act.wait_ge(rest1_ready, i + 1)
                    nc.scalar.activation(parts[:, 1], r1, ACT.Copy).then_inc(part2_ready, 1)
                if ends(i):
                    for t, bank in enumerate((PA[:, 1, :], PB[:, 0, :])):
                        act.wait_ge(act_T_done, i * LT - LT + t + 1)
                        nc.scalar.activation(act_qT[:, t].rearrange("p c n -> p (c n)"), bank.bitcast(bf16), ACT.Copy)\
                            .then_inc(act_qT_ready, 1)
                if follows(i):
                    take_oT(i + 1)
                if ends(i):
                    rstd_of(2, i - 1)

            batches(act, tail)

        @block.vector
        def _(dve):
            nc.vector.memset(eps_rms[:, :], RMS_EPS).then_inc(eps_ready, 1)
            nc.vector.memset(eps_ln[:, :], LN_EPS).then_inc(eps_ready, 1)
            dve.wait_ge(xT_in, 48)
            nc.vector.scalar_tensor_tensor(wqk[:, :], qn_sb[:, :], SCALE, kn_sb[:, :], ALU.mult, ALU.mult)\
                .then_inc(wqk_ready, 1)
            dve.wait_ge(ssm_in, 32)
            nc.vector.tensor_tensor(win, cw_sb, in_sb.unsqueeze(1).to_broadcast([P, TAPS, DI]), ALU.mult)\
                .then_inc(win_ready, 1)
            dve.wait_ge(small_in, 16 * 6)
            nc.vector.tensor_scalar(ncb[:, :], cb_sb[:, :], -1.0, None, ALU.mult).then_inc(ncb_ready, 1)
            dve.wait_ge(expA_ready, 1)
            nc.vector.tensor_scalar(A[:, :, :], expA[:, :, :], -1.0, None, ALU.mult).then_inc(A_ready, 1)

            def take_k(s, b):
                dve.wait_ge(rinv_ready, s + 1)
                dve.wait_ge(qk_raw_ready, s + 1)
                for t in range(LT):
                    r = t * (REP + 1) + REP
                    last = nc.vector.tensor_scalar(qk_raw[:, t, REP * HD:], qk_raw[:, t, REP * HD:],
                                                   rinv[:, b % 2, r:r + 1], None, ALU.mult)
                last.then_inc(k_norm_ready, 1)

            def take_kT(s):
                dve.wait_ge(qkT_done, s + 1)
                nc.vector.tensor_scalar(kT[:, :], PB[:, 1, 0:L], wqk[:, 0:1], None, ALU.mult).then_inc(kT_ready, 1)

            def take_pT(s):
                dve.wait_ge(pT_done, s + 1)
                nc.vector.tensor_copy(pT[:, 1], PD[:, 1, :]).then_inc(pT_half1, 1)

            def take_attn(g, b, s):
                dve.wait_ge(pv_done, s + 1)
                nc.vector.tensor_copy(attnT[:, bass.ds(g * REP, REP), b * L:(b + 1) * L],
                                      PD[:, 0, :].rearrange("p (j l) -> p j l", j=REP)).then_inc(attn_ready, 1)

            def input_of(k, n, b):
                dve.wait_ge(bc_loaded[b // 2], n * 16)
                nc.vector.tensor_tensor(dBu, du[:, b % 2], bc[:, b // 2, 0], ALU.mult).then_inc(dBu_ready, 1)

            def scan(k, b):
                dve.wait_ge(dBu_ready, k + 1)
                dve.wait_ge(dA_ready, k + 1)
                nc.vector.tensor_tensor_scan(st, dA[:, b % 2].rearrange("p b l -> p (b l)"), dBu, 0.0,
                                             ALU.mult, ALU.add).then_inc(dA_free, 1)

            def output_of(k, b):
                dve.wait_ge(dA_free, k + 3)
                dve.wait_ge(y_added, k + 1)
                nc.vector.tensor_tensor(prod[:, b % 2], st, bc[:, b // 2, 1], ALU.mult).then_inc(prod_ready, 1)

            def silu(b):
                at = slice(b * L, (b + 1) * L)
                dve.wait_ge(expv_ready, (b + 1) * DC)
                nc.vector.tensor_scalar(du[:, :, at], dt[:, :, at], 1.0, None, ALU.add).then_inc(den_ready, 1)
                dve.wait_ge(den_ready, b + 1)
                nc.vector.reciprocal(dt[:, :, at], du[:, :, at]).then_inc(sig_ready, 1)
                dve.wait_ge(sig_ready, b + 1)
                for i in range(DC):
                    last = nc.vector.scalar_tensor_tensor(u[:, i, at], PA[:, 1, i * L:(i + 1) * L], cb_sb[:, i:i + 1],
                                                          dt[:, i, at], ALU.add, ALU.mult)
                last.then_inc(u_ready, 1)

            def take_xdbl(b):
                dve.wait_ge(xdbl_done, b + 1)
                nc.vector.tensor_copy(xdbl[:, b * L:(b + 1) * L], PB[0:BC + RANK, 1, L:2 * L]).then_inc(xdbl_ready, 1)

            def softplus_rest(b):
                at = slice(b * L, (b + 1) * L)
                dve.wait_ge(sp_exp, b + 1)
                nc.vector.tensor_scalar(y[:, :, at], du[:, :, at], 1.0, -1.0, ALU.add, ALU.add).then_inc(sp_w1, 1)
                dve.wait_ge(sp_w1, b + 1)
                nc.vector.tensor_tensor(lost, du[:, :, at], y[:, :, at], ALU.subtract).then_inc(sp_lost, 1)
                dve.wait_ge(sp_lost, b + 1)
                dve.wait_ge(sp_relu, (b + 1) * DC)
                nc.vector.tensor_tensor(dt[:, :, at], dt[:, :, at], lost, ALU.add).then_inc(sp_rest, 1)

            def softplus_end():
                for i in range(DC):
                    dve.wait_ge(sp_ln, i + 1)
                    dve.wait_ge(sp_w1, B)
                    nc.vector.scalar_tensor_tensor(ln_out[:, i], y[:, i], 0.0, ln_out[:, i], ALU.is_gt, ALU.mult)\
                        .then_inc(sp_gate, 1)
                    dve.wait_ge(sp_gate, i + 1)
                    dve.wait_ge(sp_rest, B)
                    nc.vector.tensor_tensor(dt[:, i], dt[:, i], ln_out[:, i], ALU.add).then_inc(dt_ready, 1)
                dve.wait_ge(du_ready, DC)

            def ternary(k, w, q, part):
                if part == 0:
                    dve.wait_ge((fc_in, pr_in)[k], 16)
                    nc.vector.tensor_reduce(asum[:, k:k + 1], w, AX.XY, ALU.add, apply_absolute_value=True)\
                        .then_inc(abs_ready, 1)
                elif part == 1:
                    dve.wait_ge(abs_summed, k + 1)
                    nc.vector.tensor_scalar(wscale[:, k:k + 1], atot[:, k:k + 1], 1.0 / (HID * FF), Q_EPS,
                                            ALU.mult, ALU.max).then_inc(wscale_ready, 1)
                    dve.wait_ge(wscale_ready, k + 1)
                    nc.vector.reciprocal(winv[:, k:k + 1], wscale[:, k:k + 1]).then_inc(winv_ready, 1)
                    if k == 0:
                        nc.vector.tensor_scalar(up_c[:, :], wscale[:, 0:1], wscale[:, 0:1], LEVELS,
                                                ALU.mult, ALU.mult).then_inc(up_ready, 1)
                    else:
                        nc.vector.tensor_scalar(down_c[:, :], wscale[:, 1:2], 1.0 / LEVELS, None, ALU.mult)\
                            .then_inc(up_ready, 1)
                    dve.wait_ge(winv_ready, k + 1)
                    nc.vector.tensor_scalar(w, w, winv[:, k:k + 1], ROUND, ALU.mult, ALU.add).then_inc(w_scaled, 1)
                elif part == 2:
                    dve.wait_ge(w_scaled, k + 1)
                    nc.vector.tensor_scalar(w, w, -ROUND, 1.0, ALU.add, ALU.min).then_inc(w_clipped, 1)
                else:
                    dve.wait_ge(w_clipped, k + 1)
                    dve.wait_ge(proj_done, STEPS * LT)
                    nc.vector.tensor_scalar(q, w, -1.0, None, ALU.max).then_inc(ternary_ready, 1)

            take_k(0, 0)
            dve.wait_ge(wqk_ready, 1)
            take_kT(0)

            def body(g):
                for b in range(B):
                    s = g * B + b
                    first = fixed(g) and g == 0
                    dve.wait_ge(scores_done, s + 1)
                    nc.vector.tensor_reduce(mx[:, :], PC[:, :, :].rearrange("p t (j k) -> p (t j) k", j=REP), AX.X,
                                            ALU.max).then_inc(mx_ready, 1)
                    if has_step(g, b, 1):
                        take_k(s + 1, b + 1)
                    dve.wait_ge(mx_ready, s + 1)
                    nc.vector.scalar_tensor_tensor(
                        nbias[:, b % 2].rearrange("p (t j) -> p t j", t=LT), mx[:, :].rearrange("p (t j) -> p t j", t=LT),
                        -1.0, rinv[:, b % 2].rearrange("p (t j) -> p t j", t=LT)[:, :, 0:REP], ALU.mult, ALU.mult)\
                        .then_inc(nbias_ready, 1)
                    if first:
                        silu(b)
                    else:
                        input_of(s - B, g, b)
                    if has_step(g, b, -1):
                        take_pT(s - 1)
                    if has_step(g, b, 1):
                        take_kT(s + 1)
                    if first:
                        take_xdbl(b)
                    else:
                        scan(s - B, b)
                    dve.wait_ge(exp_done, s + 1)
                    nc.vector.reciprocal(rsinv[:, b % 2], rowsum[:, b % 2]).then_inc(rsinv_ready, 1)
                    if has_step(g, b, -1):
                        take_attn(*((g, b - 1) if b else (g - 1, B - 1)), s - 1)
                    if first:
                        softplus_rest(b)
                    else:
                        output_of(s - B, b)
                    if fixed(g) and g == KV_HEADS - 1:
                        ternary(0, fc_sb, w1q, b)
                if first:
                    softplus_end()

            groups(dve, body)

            def normalize(k, b, src, dst):
                for t in range(LT):
                    last = nc.vector.bn_stats(stats[:, k, t], src[:, t])
                last.then_inc(stats_ready[k], 1)
                dve.wait_ge(eps_ready, 2)
                dve.wait_ge(stats_ready[k], b + 1)
                for t in range(LT):
                    last = nc.vector.bn_aggr(mv[:, k, t], stats[:, k, t])
                last.then_inc(mv_ready[k], 1)
                dve.wait_ge(rstd_ready[k], b + 1)
                for t in range(LT):
                    last = nc.vector.tensor_scalar(dst[:, t], src[:, t], mv[:, k, t, 0:1], rstd[:, k, t:t + 1],
                                                   ALU.subtract, ALU.mult)
                last.then_inc(xn_ready[k], 1)

            def activate(b):
                for t, bank in enumerate((PC, PD)):
                    n = b * LT + t + 1
                    dve.wait_ge(up_done, n)
                    nc.vector.tensor_scalar(act_sq[:, t], bank[:, :, :].rearrange("p a n -> p (a n)"), 0.0, None,
                                            ALU.max, ALU.max, accum_out=hmax[:, t:t + 1]).then_inc(relu_ready, 1)
                dve.wait_ge(relu_ready, b * LT + LT)
                nc.vector.tensor_scalar(hs[:, :], hmax[:, :], wscale[:, 0:1], None, ALU.mult).then_inc(hs_ready, 1)
                dve.wait_ge(hs_ready, b + 1)
                nc.vector.tensor_tensor(hs2[:, :], hs[:, :], hs[:, :], ALU.mult).then_inc(hs2_ready, 1)
                dve.wait_ge(hs2_ready, b + 1)
                nc.vector.tensor_scalar(xmax[:, :], hs2[:, :], Q_EPS, None, ALU.max).then_inc(xmax_ready, 1)
                dve.wait_ge(xmax_ready, b + 1)
                nc.vector.reciprocal(xinv[:, :], xmax[:, :]).then_inc(xinv_ready, 1)
                nc.vector.tensor_scalar(o_mul[:, :], xmax[:, :], down_c[:, 0:1], None, ALU.mult).then_inc(mul_ready, 1)
                dve.wait_ge(xinv_ready, b + 1)
                nc.vector.tensor_scalar(q_mul[:, :], xinv[:, :], up_c[:, 0:1], None, ALU.mult).then_inc(mul_ready, 1)

            def levels(b):
                dve.wait_ge(mul_ready, b * 2 + 2)
                for t in range(LT):
                    dve.wait_ge(sq_ready, b * LT + t + 1)
                    nc.vector.tensor_scalar(act_sq[:, t], act_sq[:, t], q_mul[:, t:t + 1], ROUND, ALU.mult, ALU.add)\
                        .then_inc(rounded, 1)
                for t in range(LT):
                    dve.wait_ge(rounded, b * LT + t + 1)
                    nc.vector.tensor_scalar(act_q[:, t], act_sq[:, t], -ROUND, None, ALU.add).then_inc(act_q_ready, 1)

            def tail(i):
                if begins(i):
                    if fixed(i) and i == 0:
                        dve.wait_ge(x_in, 16)
                    dve.wait_ge(back_done, i + 1)
                    nc.vector.tensor_tensor(x1p, PA[:, 1, :].rearrange("p (t n) -> p t n", t=LT),
                                            x_sb[:, bass.ds(i * LT, LT)], ALU.add).then_inc(xp_ready[0], 1)
                    dve.wait_ge(xp_ready[0], i + 1)
                    normalize(0, i, x1p, x1)
                if fixed(i) and i == 0:
                    take_pT(STEPS - 1)
                    for b in range(B):
                        input_of(STEPS - B + b, KV_HEADS, b)
                        if b == 2:
                            take_attn(KV_HEADS - 1, B - 1, STEPS - 1)
                        scan(STEPS - B + b, b)
                        output_of(STEPS - B + b, b)
                if begins(i):
                    dve.wait_ge(ez_ready, i + 1)
                    nc.vector.tensor_scalar(ex, ex, 1.0, None, ALU.add).then_inc(ez1_ready, 1)
                    dve.wait_ge(ez1_ready, i + 1)
                    nc.vector.reciprocal(ex, ex).then_inc(sz_ready, 1)
                    dve.wait_ge(sz_ready, i + 1)
                    nc.vector.tensor_tensor(ex, ex, x1, ALU.mult).then_inc(z_ready, 1)
                    if fixed(i) and i == 0:
                        dve.wait_ge(y_added, STEPS + DC)
                    dve.wait_ge(z_ready, i + 1)
                    nc.vector.tensor_tensor(gated, ex, y[:, :, bass.ds(i * L, L)], ALU.mult).then_inc(gated_ready, 1)
                if fixed(i) and i == 0:
                    for part in range(2):
                        ternary(1, pr_sb, w2q, part)
                if ends(i):
                    activate(i - 1)
                if begins(i):
                    dve.wait_ge(gT_done, i + 1)
                    nc.vector.tensor_tensor(x2p, PB[:, 0, :].rearrange("p (t n) -> p t n", t=LT), x1, ALU.add)\
                        .then_inc(xp_ready[1], 1)
                    dve.wait_ge(xp_ready[1], i + 1)
                    normalize(1, i, x2p, x2)
                if ends(i):
                    levels(i - 1)
                if begins(i):
                    dve.wait_ge(part1_ready, i + 1)
                    nc.vector.tensor_tensor(r1, PB[:, 1, :].rearrange("p (c n) -> p c n", c=HC), parts[:, 0],
                                            ALU.subtract).then_inc(rest1_ready, 1)
                    dve.wait_ge(part2_ready, i + 1)
                    nc.vector.tensor_tensor(parts[:, 2], r1, parts[:, 1], ALU.subtract).then_inc(part3_ready, 1)
                if fixed(i) and i == 0:
                    for part in range(2, 4):
                        ternary(1, pr_sb, w2q, part)
                if ends(i):
                    dve.wait_ge(down_done, i * LT)
                    for t in range(LT):
                        last = nc.vector.scalar_tensor_tensor(x3p[:, t], PB[:, 1, t * HID:(t + 1) * HID],
                                                              o_mul[:, t:t + 1], x2_kept[:, t], ALU.mult, ALU.add)
                    last.then_inc(xp_ready[2], 1)
                    dve.wait_ge(xp_ready[2], i)
                if begins(i):
                    dve.wait_ge(xn_ready[1], i + 1)
                    nc.vector.tensor_copy(x2_kept, x2).then_inc(kept, 1)
                if ends(i):
                    if not fixed(i) or i > 1:
                        reach(dve, stored, i * 16 - 16)
                    normalize(2, i - 1, x3p, x3)
                if begins(i):
                    dve.wait_ge(kept, i + 1)

            batches(dve, tail)

        @block.tensor
        def _(pe):
            def project_tile(g, b, t):
                for c in range(HC):
                    last = nc.tensor.matmul(PA[:, t, :], xT_sb[:, c, b * L + t * P:b * L + (t + 1) * P],
                                            w_sb[:, bass.ds(g, 1), c].rearrange("p o n -> p (o n)"),
                                            start=(c == 0), stop=(c == HC - 1))
                last.then_inc(proj_done, 1)

            def transpose_qk(s):
                pe.wait_ge(qk_raw_ready, s + 1)
                pe.wait_ge(k_norm_ready, s + 1)
                for j in range(REP + 1):
                    dst = PB[:, 0, j * L:(j + 1) * L] if j < REP else PB[:, 1, 0:L]
                    for t in range(LT):
                        last = nc.tensor.transpose(dst[:, t * P:(t + 1) * P], qk_raw[:, t, j * HD:(j + 1) * HD],
                                                   ident[:, :])
                last.then_inc(qkT_done, 1)

            def scores(s):
                pe.wait_ge(qT_ready, s + 1)
                pe.wait_ge(kT_ready, s + 1)
                reach(pe, exp_done, s)
                for t in range(LT):
                    for j in range(REP):
                        windowed = t * P >= L - WINDOW
                        last = nc.tensor.matmul(PC[:, t, j * L:(j + 1) * L], qT[:, j * L + t * P:j * L + (t + 1) * P],
                                                kT[:, :], start=True, stop=not windowed)
                        if windowed:
                            last = nc.tensor.matmul(PC[:, t, j * L + P:(j + 1) * L], ident16[:, :], mask16[:, :],
                                                    start=False, stop=True)
                last.then_inc(scores_done, 1)

            def transpose_probs(s, b):
                pe.wait_ge(normed, s + 1)
                reach(pe, attn_ready, s)
                for c in range(LT):
                    for j in range(REP):
                        for t in range(LT):
                            last = nc.tensor.transpose(PD[:, c, j * L + t * P:j * L + (t + 1) * P],
                                                       probs[:, b % 2, t, j, c * P:(c + 1) * P], ident[:, :])
                last.then_inc(pT_done, 1)

            def attend(s, b):
                pe.wait_ge(pT_half0, s + 1)
                pe.wait_ge(pT_half1, s + 1)
                for c in range(LT):
                    last = nc.tensor.matmul(PD[:, 0, :], v_sb[:, b % 4, c], pT[:, c], start=(c == 0), stop=(c == LT - 1))
                last.then_inc(pv_done, 1)

            def convolve(b):
                if b == 0:
                    pe.wait_ge(win_ready, 1)
                    pe.wait_ge(ctx_in, 16)
                pe.wait_ge(qk_raw_ready, b + 2)
                pe.wait_ge(v_ready, b + 2)
                for i in range(DC):
                    for k in range(TAPS):
                        last = nc.tensor.matmul(PA[:, 1, i * L:(i + 1) * L], win[:, k, i * P:(i + 1) * P],
                                                ctxp[:, b, k:k + L], start=(k == 0), stop=(k == TAPS - 1))
                last.then_inc(conv_done, 1)

            def x_proj(b):
                pe.wait_ge(small_in, 16 * 6)
                pe.wait_ge(u_ready, b + 1)
                pe.wait_ge(kT_ready, b + 2)
                for i in range(DC):
                    last = nc.tensor.matmul(PB[0:BC + RANK, 1, L:2 * L], xp_sb[:, i], u[:, i, b * L:(b + 1) * L],
                                            start=(i == 0), stop=(i == DC - 1))
                last.then_inc(xdbl_done, 1)

            def dt_proj(b):
                pe.wait_ge(xdbl_ready, b + 1)
                for i in range(DC):
                    last = nc.tensor.matmul(PA[:, 1, i * L:(i + 1) * L], dtw_sb[BC:, i * P:(i + 1) * P],
                                            xdbl[BC:, b * L:(b + 1) * L], start=True, stop=True)
                last.then_inc(dt_done, 1)

            def out_project(b, quarter):
                if quarter == 0:
                    pe.wait_ge(attn_ready, b + (STEPS - B + 1))
                n = HC * HEADS // 4
                for k in range(quarter * n, (quarter + 1) * n):
                    c, h = k // HEADS, k % HEADS
                    last = nc.tensor.matmul(PA[:, 0, c * L:(c + 1) * L], wo_sb[:, h, c * P:(c + 1) * P],
                                            attnT[:, h, bass.ds(b * L, L)], start=(h == 0), stop=(h == HEADS - 1))
                if quarter == 3:
                    last.then_inc(wo_done, 1)

            pe.wait_ge(xT_in, 48)
            pe.wait_ge(w_in[0], 16)
            for t in range(LT):
                project_tile(0, 0, t)
            pe.wait_ge(const_ready, 3)
            transpose_qk(0)
            pe.wait_ge(v_ready, 1)
            for t in range(LT):
                project_tile(0, 1, t)

            def body(g):
                for b in range(B):
                    s = g * B + b
                    first = fixed(g) and g == 0
                    final = fixed(g) and g == KV_HEADS - 1
                    scores(s)
                    if first:
                        convolve(b)
                    if has_step(g, b, -1):
                        transpose_probs(s - 1, b + 1)
                    if has_step(g, b, 1):
                        transpose_qk(s + 1)
                    if first:
                        x_proj(b)
                    ahead_g, ahead_b = (g, b + 2) if b + 2 < B else (g + 1, b + 2 - B)
                    if has_step(g, b, 2):
                        if b + 2 == B:
                            if first:
                                pe.wait_ge(w_in[1], 16)
                            else:
                                pe.wait_ge(w_rest, g * 16)
                        pe.wait_ge(v_ready, s + 2)
                        project_tile(ahead_g, ahead_b, 0)
                    elif b == 2:
                        pe.wait_ge(v_ready, STEPS)
                        pe.wait_ge(wo_in, 16)
                        out_project(0, 0)
                    else:
                        out_project(0, 2)
                    if has_step(g, b, -1):
                        attend(s - 1, b + 3)
                    if first:
                        dt_proj(b)
                        pe.wait_ge(sp_relu, (b + 1) * DC)
                        pe.wait_ge(sp_abs, (b + 1) * DC)
                    if has_step(g, b, 2):
                        project_tile(ahead_g, ahead_b, 1)
                    elif b == 2:
                        out_project(0, 1)
                    else:
                        out_project(0, 3)

            groups(pe, body)

            def tail(i):
                if begins(i):
                    pe.wait_ge(oT_ready, i + 1)
                    for t in range(LT):
                        for c in range(HC):
                            last = nc.tensor.transpose(PA[:, 1, t * HID + c * P:t * HID + (c + 1) * P],
                                                       oT[:, c, t * P:(t + 1) * P], ident[:, :])
                    last.then_inc(back_done, 1)
                if follows(i):
                    out_project(i + 1, 0)
                if fixed(i) and i == 0:
                    transpose_probs(STEPS - 1, B - 1)
                if ends(i):
                    pe.wait_ge(attn_ready, STEPS)
                    pe.wait_ge(ternary_ready, 1)
                    pe.wait_ge(part3_ready, i)
                    for t, bank in enumerate((PC, PD)):
                        for half in range(2):
                            for k in range(3 * HC):
                                last = nc.tensor.matmul(bank[:, half, :], parts[:, k // HC, k % HC, t * P:(t + 1) * P],
                                                        w1q[:, k % HC, half * 512:(half + 1) * 512],
                                                        start=(k == 0), stop=(k == 3 * HC - 1))
                        last.then_inc(up_done, 1)
                if fixed(i) and i == 0:
                    out_project(i + 1, 1)
                    attend(STEPS - 1, B - 1)
                    out_project(i + 1, 2)
                if begins(i):
                    pe.wait_ge(gated_ready, i + 1)
                    for t in range(LT):
                        for c in range(DC):
                            last = nc.tensor.transpose(PB[:, 0, t * DI + c * P:t * DI + (c + 1) * P],
                                                       gated[:, c, t * P:(t + 1) * P], ident[:, :])
                    last.then_inc(gT_done, 1)
                if follows(i) and not (fixed(i) and i == 0):
                    out_project(i + 1, 1)
                if fixed(i) and i == 0:
                    out_project(i + 1, 3)
                if begins(i):
                    pe.wait_ge(xn_ready[1], i + 1)
                    for c in range(HC):
                        for t in range(LT):
                            last = nc.tensor.transpose(PB[:, 1, c * L + t * P:c * L + (t + 1) * P],
                                                       x2[:, t, c * P:(c + 1) * P], ident[:, :])
                    last.then_inc(x2T_done, 1)
                if follows(i) and not (fixed(i) and i == 0):
                    out_project(i + 1, 2)
                if ends(i):
                    for t, bank in enumerate((PA[:, 1, :], PB[:, 0, :])):
                        pe.wait_ge(act_q_ready, i * LT - LT + t + 1)
                        for c in range(FC):
                            last = nc.tensor.transpose(bank.bitcast(bf16)[:, c * P:(c + 1) * P],
                                                       act_q[:, t, c * P:(c + 1) * P], ident16[:, :])
                        last.then_inc(act_T_done, 1)
                if follows(i) and not (fixed(i) and i == 0):
                    out_project(i + 1, 3)
                if ends(i):
                    pe.wait_ge(ternary_ready, 2)
                    if begins(i):
                        pe.wait_ge(part3_ready, i + 1)
                    for t in range(LT):
                        pe.wait_ge(act_qT_ready, i * LT - LT + t + 1)
                        for c in range(FC):
                            last = nc.tensor.matmul(PB[:, 1, t * HID:(t + 1) * HID], act_qT[:, t, c], w2q[:, c],
                                                    start=(c == 0), stop=(c == FC - 1))
                        last.then_inc(down_done, 1)

            batches(pe, tail)


def kernel(**inputs):
    import numpy as np
    import concourse.bacc as bacc
    from concourse.bass_utils import run_bass_kernel_spmd

    def two(a, rows, cols):
        return a.reshape(rows, cols).T

    a = {k: np.asarray(v) for k, v in inputs.items()}
    x = a["x"].reshape(T, HID)
    wq = a["L0_attn_Wq"].reshape(KV_HEADS, REP * HD, HID)
    wk = a["L0_attn_Wk"].reshape(KV_HEADS, HD, HID)
    wv = a["L0_attn_Wv"].reshape(KV_HEADS, HD, HID)
    xp = a["L0_xattn_x_proj_w"]
    b_rows, c_rows = xp[RANK:RANK + NS], xp[RANK + NS:]
    bc_rows = np.stack([b_rows, c_rows], axis=1).reshape(BC, DI)
    named = {
        "x": x,
        "xT": x.T,
        "ctxT": a["ctx_1024"].reshape(T, CTX).T,
        "w_qkvT": np.concatenate([wq, wk, wv], axis=1).transpose(0, 2, 1),
        "w_oT": a["L0_attn_Wo"].T,
        "q_norm": a["L0_attn_q_norm_w"].reshape(HD, 1),
        "k_norm": a["L0_attn_k_norm_w"].reshape(HD, 1),
        "in_projT": a["L0_xattn_in_proj_w"].T,
        "conv_wT": a["L0_xattn_conv_w"].reshape(DI, TAPS).T,
        "conv_b": two(a["L0_xattn_conv_b"], DC, P),
        "x_projT": np.concatenate([bc_rows, xp[:RANK]], axis=0).T,
        "dt_projT": a["L0_xattn_dt_proj_w"].T,
        "dt_b": two(a["L0_xattn_dt_proj_b"], DC, P),
        "a_log": a["L0_xattn_A_log"],
        "d_skip": two(a["L0_xattn_D"], DC, P),
        "c_fc": a["L0_ffn_c_fc"],
        "c_projT": a["L0_ffn_c_proj"].T,
    }
    nc = bacc.Bacc("TRN2", target_bir_lowering=False, num_devices=1)
    arrays, args = {}, []
    for name, v in named.items():
        v = np.ascontiguousarray(v)
        arrays[f"in_{name}"] = v
        args.append(nc.dram_tensor(f"in_{name}", v.shape, mybir.dt.from_np(v.dtype), kind="ExternalInput").ap())
    args.append(nc.dram_tensor("layer_out", (T, HID), mybir.dt.float32, kind="ExternalOutput").ap())
    decoder_layer(nc, *args)
    r = run_bass_kernel_spmd(nc, [arrays], core_ids=[0])
    return r.results[0]["layer_out"].reshape(B, L, HID)
```

```python
import concourse.bass as bass
from concourse import mybir
from contextlib import ExitStack

B, L, HID = 4, 256, 256
T = B * L
P = 128
HEADS, KV_HEADS, HD = 16, 8, 128
REP = HEADS // KV_HEADS
WINDOW = 128
CTX = 128
DI, NS, RANK, TAPS = 256, 16, 8, 4
FF = 1024
LT = L // P
HC = HID // P
DC = DI // P
FC = FF // P
GW = (REP + 2) * HD
STEPS = KV_HEADS * B
BC = 2 * NS
RMS_EPS, LN_EPS, Q_EPS = 1e-6, 1e-5, 1e-5
SCALE = float(HD) ** -0.5
LEVELS = 255.0
ROUND = 1.5 * 2.0 ** 23
MASKED = -1e30
PART_SCALE = 1024.0


def decoder_layer(nc, x, xT, ctxT, w_qkvT, w_oT, q_norm, k_norm, in_projT, conv_wT, conv_b, x_projT,
                  dt_projT, dt_b, a_log, d_skip, c_fc, c_projT, out):
    f32, bf16, f16 = mybir.dt.float32, mybir.dt.bfloat16, mybir.dt.float16
    ALU = mybir.AluOpType
    ACT = mybir.ActivationFunctionType
    AX = mybir.AxisListType

    ctx = ExitStack()
    with ctx:
        def sb(name, shape, dt=f32):
            return ctx.enter_context(nc.sbuf_tensor(name, shape, dt))

        def sem(name):
            return ctx.enter_context(nc.semaphore(name))

        xT_sb = sb("xT_sb", [P, HC, T])
        w_sb = sb("w_sb", [P, KV_HEADS, HC, GW])
        attnT = sb("attnT", [P, HEADS, T])
        u = sb("u", [P, DC, T])
        dt = sb("dt", [P, DC, T])
        du = sb("du", [P, DC, T])
        y = sb("y", [P, DC, T])
        work = sb("work", [P, 10 * T])

        w_flat = w_sb[:, :, :, :].rearrange("p g c n -> p (g c n)")
        wo_sb = w_flat[:, 0:HEADS * HID].rearrange("p (h n) -> p h n", h=HEADS)
        fc_sb = w_flat[:, 4096:6144].rearrange("p (c n) -> p c n", c=HC)
        pr_sb = w_flat[:, 6144:8192].rearrange("p (c n) -> p c n", c=FC)
        x_sb = u[:, :, :].rearrange("p c t -> p (c t)").rearrange("p (i n) -> p i n", n=HID)
        early = attnT[:, HEADS // 2:, :].rearrange("p h t -> p (h t)")
        ctxp = early[:, 0:B * (TAPS - 1 + L)].rearrange("p (b l) -> p b l", b=B)
        in_sb = early[:, 1280:1280 + DI]
        cw_sb = early[:, 2048:2048 + TAPS * DI].rearrange("p (k e) -> p k e", k=TAPS)
        win = early[:, 3072:3072 + TAPS * DI].rearrange("p (k e) -> p k e", k=TAPS)
        xdbl = early[0:BC + RANK, 4096:4096 + T]
        dtw_sb = early[0:BC + RANK, 5120:5120 + DI]
        xp_sb = early[:, 6144:6144 + DC * (BC + RANK)].rearrange("p (c n) -> p c n", c=DC)
        lost = early[:, 6912:6912 + DC * L].rearrange("p (c l) -> p c l", c=DC)
        ln_out = early[:, 2048:2048 + DC * T].rearrange("p (c t) -> p c t", c=DC)
        bc = work[:, 0:4 * T].rearrange("p (s k t) -> p s k t", s=2, k=2)
        dA = work[:, 4 * T:6 * T].rearrange("p (s b l) -> p s b l", s=2, b=B)
        dBu = work[:, 6 * T:7 * T]
        st = work[:, 7 * T:8 * T]
        prod = work[:, 8 * T:10 * T].rearrange("p (s t) -> p s t", s=2)
        cb_sb = sb("cb_sb", [P, DC])
        dtb_sb = sb("dtb_sb", [P, DC])
        alog_sb = sb("alog_sb", [P, DC, NS])
        d_sb = sb("d_sb", [P, DC])
        qn_sb = sb("qn_sb", [P, 1])
        kn_sb = sb("kn_sb", [P, 1])
        ident = sb("ident", [P, P])
        ident16 = sb("ident16", [P, P], bf16)
        mask16 = sb("mask16", [P, P], bf16)
        eps_rms = sb("eps_rms", [P, 1])
        eps_ln = sb("eps_ln", [P, 1])
        A = sb("A", [P, DC, NS])
        expA = sb("expA", [P, DC, NS])
        qk_raw = sb("qk_raw", [P, LT, (REP + 1) * HD])
        square = sb("square", [P, LT, REP + 1, HD], bf16)
        ssq = sb("ssq", [P, 2, LT * (REP + 1)])
        lnr = sb("lnr", [P, 2, LT * (REP + 1)])
        rinv = sb("rinv", [P, 2, LT * (REP + 1)])
        wqk = sb("wqk", [P, 1])
        v_sb = sb("v_sb", [P, 4, LT, HD])
        qT = sb("qT", [P, REP * L])
        kT = sb("kT", [P, L])
        mx = sb("mx", [P, LT * REP])
        nbias = sb("nbias", [P, 2, LT * REP])
        rowsum = sb("rowsum", [P, 2, LT * REP])
        rsinv = sb("rsinv", [P, 2, LT * REP])
        probs = sb("probs", [P, 2, LT, REP, L])
        pT = sb("pT", [P, LT, REP * L])
        def tiles(region):
            return region.rearrange("p (t n) -> p t n", t=LT)

        probs_flat = probs[:, 0].rearrange("p t j l -> p (t j l)")
        pT_flat = pT[:, :, :].rearrange("p t l -> p (t l)")
        oT, x1p = tiles(probs_flat[:, 0:512]), tiles(probs_flat[:, 512:1024])
        gated, x2p = tiles(pT_flat[:, 0:512]), tiles(pT_flat[:, 512:1024])
        x1 = tiles(qk_raw[:, :, :].rearrange("p t n -> p (t n)")[:, 0:512])
        gate = tiles(v_sb[:, 0:2].rearrange("p s t n -> p (s t n)"))
        x2, x2_kept, x3p, x3 = (tiles(work[:, 512 * k:512 * (k + 1)]) for k in range(4))
        act_sq = tiles(work[:, 5120:7168])
        act_q = tiles(work[:, 7168:8192].bitcast(bf16))
        act_qT = work[:, 8192:9216].bitcast(bf16).rearrange("p (t c n) -> p t c n", t=LT, c=FC)
        parts = work[:, 9216:9728].bitcast(f16).rearrange("p (i c n) -> p i c n", i=2, c=HC)
        w1q = xT_sb[:, 0, :].bitcast(f16).rearrange("p (c n) -> p c n", c=HC)
        w2q = xT_sb[:, 1, :].bitcast(bf16).rearrange("p (c n) -> p c n", c=FC)
        stats = sb("stats", [P, 3, LT, 6])
        mv = sb("mv", [P, 3, LT, 2])
        lnv = sb("lnv", [P, 3, LT])
        rstd = sb("rstd", [P, 3, LT])
        asum = sb("asum", [P, 2])
        atot = sb("atot", [P, 2])
        wscale = sb("wscale", [P, 2])
        winv = sb("winv", [P, 2])
        up_c = sb("up_c", [P, 1])
        down_c = sb("down_c", [P, 1])
        hmax = sb("hmax", [P, LT])
        hs = sb("hs", [P, LT])
        hs2 = sb("hs2", [P, LT])
        xmax = sb("xmax", [P, LT])
        xinv = sb("xinv", [P, LT])
        q_mul = sb("q_mul", [P, LT])
        o_mul = sb("o_mul", [P, LT])

        PA = ctx.enter_context(nc.psum_tensor("PA", [P, 2, 512], f32))
        PB = ctx.enter_context(nc.psum_tensor("PB", [P, 2, 512], f32))
        PC = ctx.enter_context(nc.psum_tensor("PC", [P, 2, 512], f32))
        PD = ctx.enter_context(nc.psum_tensor("PD", [P, 2, 512], f32))

        bc_dram = nc.dram_tensor("bc_scratch", [NS, 2, T], f32, kind="Internal").ap()

        ctx_in = sem("ctx_in")
        ssm_in = sem("ssm_in")
        small_in = sem("small_in")
        xT_in = sem("xT_in")
        w_in = [sem("w0_in"), sem("w1_in")]
        w_rest = sem("w_rest")
        wo_in = sem("wo_in")
        fc_in = sem("fc_in")
        pr_in = sem("pr_in")
        x_in = sem("x_in")
        zeroed = sem("zeroed")
        const_ready = sem("const_ready")
        win_ready = sem("win_ready")
        conv_done = sem("conv_done")
        sig_ready = sem("sig_ready")
        u_ready = sem("u_ready")
        xdbl_done = sem("xdbl_done")
        xdbl_ready = sem("xdbl_ready")
        dt_done = sem("dt_done")
        sp_abs = sem("sp_abs")
        sp_relu = sem("sp_relu")
        sp_exp = sem("sp_exp")
        sp_w1 = sem("sp_w1")
        sp_lost = sem("sp_lost")
        sp_rest = sem("sp_rest")
        bc_stored = sem("bc_stored")
        sp_ln = sem("sp_ln")
        sp_gate = sem("sp_gate")
        dt_ready = sem("dt_ready")
        du_ready = sem("du_ready")
        expA_ready = sem("expA_ready")
        A_ready = sem("A_ready")
        bc_loaded = [sem("bc_even"), sem("bc_odd")]
        dA_free = sem("dA_free")
        dA_ready = sem("dA_ready")
        dBu_ready = sem("dBu_ready")
        prod_ready = sem("prod_ready")
        y_added = sem("y_added")
        proj_done = sem("proj_done")
        ssq_ready = sem("ssq_ready")
        ln_ready = sem("ln_ready")
        rinv_ready = sem("rinv_ready")
        v_ready = sem("v_ready")
        k_raw_ready = sem("k_raw_ready")
        q_raw_ready = sem("q_raw_ready")
        k_norm_ready = sem("k_norm_ready")
        wqk_ready = sem("wqk_ready")
        qkT_done = sem("qkT_done")
        qT_ready = sem("qT_ready")
        kT_ready = sem("kT_ready")
        scores_done = sem("scores_done")
        mx_ready = sem("mx_ready")
        nbias_ready = sem("nbias_ready")
        exp_done = sem("exp_done")
        rsinv_ready = sem("rsinv_ready")
        norm_begun = sem("norm_begun")
        normed = sem("normed")
        pT_done = sem("pT_done")
        pT_half0 = sem("pT_half0")
        pT_half1 = sem("pT_half1")
        pv_done = sem("pv_done")
        attn_ready = sem("attn_ready")

        eps_ready = sem("eps_ready")
        abs_ready = sem("abs_ready")
        abs_summed = sem("abs_summed")
        wscale_ready = sem("wscale_ready")
        winv_ready = sem("winv_ready")
        up_ready = sem("up_ready")
        w_scaled = sem("w_scaled")
        w_clipped = sem("w_clipped")
        ternary_ready = sem("ternary_ready")
        wo_done = sem("wo_done")
        oT_ready = sem("oT_ready")
        back_done = sem("back_done")
        xp_ready = [sem(f"x{k + 1}p_ready") for k in range(3)]
        stats_ready = [sem(f"stats{k + 1}_ready") for k in range(3)]
        mv_ready = [sem(f"mv{k + 1}_ready") for k in range(3)]
        lnv_ready = [sem(f"lnv{k + 1}_ready") for k in range(3)]
        rstd_ready = [sem(f"rstd{k + 1}_ready") for k in range(3)]
        xn_ready = [sem(f"x{k + 1}_ready") for k in range(3)]
        gate_ready = sem("gate_ready")
        z_ready = sem("z_ready")
        gated_ready = sem("gated_ready")
        gT_done = sem("gT_done")
        x2T_done = sem("x2T_done")
        part1_ready = sem("part1_ready")
        part2_ready = sem("part2_ready")
        up_done = sem("up_done")
        relu_ready = sem("relu_ready")
        sq_ready = sem("sq_ready")
        hs_ready = sem("hs_ready")
        hs2_ready = sem("hs2_ready")
        xmax_ready = sem("xmax_ready")
        xinv_ready = sem("xinv_ready")
        mul_ready = sem("mul_ready")
        rounded = sem("rounded")
        act_q_ready = sem("act_q_ready")
        act_T_done = sem("act_T_done")
        act_qT_ready = sem("act_qT_ready")
        down_done = sem("down_done")
        kept = sem("kept")
        stored = sem("stored")

        def reach(eng, s, value):
            if not (isinstance(value, int) and value <= 0):
                eng.wait_ge(s, value)

        def bank_of(b):
            return (PD[:, 0, :], PD[:, 1, :], PC[:, 0, :], PC[:, 1, :])[b]

        def fixed(g):
            return isinstance(g, int)

        def groups(eng, body):
            body(0)
            with eng.Fori(1, KV_HEADS - 1) as g:
                body(g)
            body(KV_HEADS - 1)

        def batches(eng, body):
            body(0)
            with eng.Fori(1, B - 1) as i:
                body(i)
            body(B - 1)
            body(B)

        def begins(i):
            return not fixed(i) or i < B

        def ends(i):
            return not fixed(i) or i > 0

        def follows(i):
            return not fixed(i) or i + 1 < B

        def final(i):
            return fixed(i) and i == B - 1

        def has_step(g, b, ahead):
            return not fixed(g) or 0 <= B * g + b + ahead < STEPS

        block = ctx.enter_context(nc.Block())

        @block.sync
        def _(sp):
            sp.dma_start(cw_sb, conv_wT.partition_broadcast(P)).then_inc(ssm_in, 16)
            sp.dma_start(ctxp[:, :, TAPS - 1:], ctxT.rearrange("c (b l) -> c b l", b=B)).then_inc(ctx_in, 16)
            sp.dma_start(xT_sb[:, :, :], xT.rearrange("(c p) t -> p c t", p=P)).then_inc(xT_in, 16)
            sp.dma_start(w_sb[:, 0], w_qkvT[0].rearrange("(c p) n -> p c n", p=P)).then_inc(w_in[0], 16)
            sp.dma_start(w_sb[:, 1], w_qkvT[1].rearrange("(c p) n -> p c n", p=P)).then_inc(w_in[1], 16)

            def load_weights(g):
                sp.dma_start(w_sb[:, bass.ds(g, 1)].rearrange("p o c n -> p (o c) n"),
                             w_qkvT[bass.ds(g, 1)].rearrange("o (c p) n -> p (o c) n", p=P)).then_inc(w_rest, 16)

            load_weights(2)
            with sp.Fori(3, KV_HEADS) as g:
                sp.wait_ge(w_rest, g * 16 - 32)
                load_weights(g)

            sp.wait_ge(xdbl_ready, B)
            sp.dma_start(bc_dram.rearrange("n k t -> (n k) t"), xdbl[0:BC, :]).then_inc(bc_stored, 16)
            sp.wait_ge(bc_stored, 16)

            def load_bc(n):
                for k in range(2):
                    reach(sp, prod_ready, B * n - B + 2 * k + 2 if not (fixed(n) and n == 0) else 0)
                    sp.dma_start(bc[:, k], bc_dram[bass.ds(n * 2 + k, 1)].rearrange("o k t -> (o k) t")
                                 .partition_broadcast(P)).then_inc(bc_loaded[k], 16)

            load_bc(0)
            sp.wait_ge(y_added, DC)
            sp.wait_ge(du_ready, DC)
            sp.dma_start(x_sb, x.rearrange("(i p) n -> p i n", p=P)).then_inc(x_in, 16)
            with sp.Fori(1, 5) as n:
                load_bc(n)
            sp.wait_ge(proj_done, 4 * B * LT)
            sp.dma_start(wo_sb, w_oT.rearrange("(h p) n -> p h n", p=P)).then_inc(wo_in, 16)
            load_bc(5)
            sp.wait_ge(proj_done, 6 * B * LT)
            sp.dma_start(fc_sb, c_fc.rearrange("(c p) n -> p c n", p=P)).then_inc(fc_in, 16)
            load_bc(6)
            load_bc(7)
            sp.wait_ge(proj_done, 8 * B * LT)
            sp.dma_start(pr_sb, c_projT.rearrange("(c p) n -> p c n", p=P)).then_inc(pr_in, 16)

            def store(b):
                sp.wait_ge(xn_ready[2], b + 1)
                sp.dma_start(out[bass.ds(b * L, L)].rearrange("(t p) n -> p t n", p=P), x3).then_inc(stored, 16)

            with sp.Fori(0, B) as b:
                store(b)
            sp.wait_ge(stored, 16 * B)

        @block.gpsimd
        def _(pool):
            nc.gpsimd.memset(ctxp[:, :, 0:TAPS - 1], 0.0).then_inc(zeroed, 1)
            nc.gpsimd.memset(ident[:, :], 0.0).then_inc(zeroed, 1)
            nc.gpsimd.memset(ident16[:, :], 0.0).then_inc(zeroed, 1)
            nc.gpsimd.memset(mask16[:, :], 0.0).then_inc(zeroed, 1)
            for k in range(2):
                nc.gpsimd.memset(dA[:, k, :, 0:1], 0.0).then_inc(dA_free, 1)
            pool.wait_ge(zeroed, 4)
            for m in (ident, ident16):
                nc.gpsimd.affine_select(out=m[:, :], in_=m[:, :], compare_op=ALU.not_equal, fill=1.0, base=0,
                                        pattern=[[-1, P]], channel_multiplier=1).then_inc(const_ready, 1)
            nc.gpsimd.affine_select(out=mask16[:, :], in_=mask16[:, :], compare_op=ALU.is_gt, fill=MASKED, base=0,
                                    pattern=[[1, P]], channel_multiplier=-1).then_inc(const_ready, 1)
            pool.wait_ge(small_in, 16 * 6)

            for i in range(DC):
                pool.wait_ge(sp_gate, i + 1)
                pool.wait_ge(u_ready, B)
                nc.gpsimd.tensor_scalar(y[:, i], u[:, i], d_sb[:, i:i + 1], 1.0, ALU.mult, ALU.mult)\
                    .then_inc(y_added, 1)

            def add_y(k, b):
                pool.wait_ge(prod_ready, k + 1)
                pool.wait_ge(y_added, k + 1)
                nc.gpsimd.tensor_tensor(y[:, b % 2], y[:, b % 2], prod[:, b % 2], ALU.add).then_inc(y_added, 1)

            def sum_abs(k):
                pool.wait_ge(abs_ready, k + 1)
                nc.gpsimd.partition_all_reduce(atot[:, k:k + 1], asum[:, k:k + 1], P, bass.bass_isa.ReduceOp.add)\
                    .then_inc(abs_summed, 1)

            def body(g):
                for b in range(B):
                    s = g * B + b
                    pool.wait_ge(rsinv_ready, s + 1)
                    pool.sem_inc(norm_begun, 1)
                    for t in range(LT):
                        for j in range(REP):
                            last = nc.gpsimd.tensor_scalar(probs[:, b % 2, t, j], probs[:, b % 2, t, j],
                                                           rsinv[:, b % 2, t * REP + j:t * REP + j + 1], 1.0,
                                                           ALU.mult, ALU.mult)
                    last.then_inc(normed, 1)
                    add_y(s, b)
                    if fixed(g) and g == KV_HEADS - 1 and b == 0:
                        sum_abs(0)

            groups(pool, body)
            sum_abs(1)

        @block.scalar
        def _(act):
            act.dma_start(in_sb, in_projT).then_inc(ssm_in, 16)
            act.dma_start(qn_sb[:, :], q_norm).then_inc(xT_in, 16)
            act.dma_start(kn_sb[:, :], k_norm).then_inc(xT_in, 16)
            for dst, src in ((cb_sb[:, :], conv_b), (xp_sb, x_projT.rearrange("(c p) n -> p c n", p=P)),
                             (dtw_sb[BC:, :], dt_projT), (dtb_sb[:, :], dt_b),
                             (alog_sb[:, :, :], a_log.rearrange("(c p) n -> p c n", p=P)), (d_sb[:, :], d_skip)):
                act.dma_start(dst, src).then_inc(small_in, 16)

            nc.scalar.preload_act_table_set("sigmoid_and_others")
            act.wait_ge(small_in, 16 * 6)
            act.wait_ge(eps_ready, 2)

            def norm(s, b):
                for t in range(LT):
                    act.wait_ge(proj_done, s * LT + t + 1)
                    for j in range(REP + 1):
                        last = nc.scalar.activation(square[:, t, j], PA[:, t, j * HD:(j + 1) * HD], ACT.Square,
                                                    accum_out=ssq[:, b % 2, t * (REP + 1) + j:t * (REP + 1) + j + 1])
                last.then_inc(ssq_ready, 1)
                nc.scalar.activation(v_sb[:, b % 4], PA[:, :, (REP + 1) * HD:], ACT.Copy).then_inc(v_ready, 1)
                act.wait_ge(ssq_ready, s + 1)
                nc.scalar.activation(lnr[:, b % 2], ssq[:, b % 2], ACT.Ln, scale=1.0 / HD, bias=eps_rms[:, :])\
                    .then_inc(ln_ready, 1)
                nc.scalar.activation(qk_raw[:, :, REP * HD:], PA[:, :, REP * HD:(REP + 1) * HD], ACT.Copy)\
                    .then_inc(k_raw_ready, 1)
                act.wait_ge(ln_ready, s + 1)
                nc.scalar.activation(rinv[:, b % 2], lnr[:, b % 2], ACT.Exp, scale=-0.5).then_inc(rinv_ready, 1)
                nc.scalar.activation(qk_raw[:, :, 0:REP * HD], PA[:, :, 0:REP * HD], ACT.Copy).then_inc(q_raw_ready, 1)

            def take_qT(s):
                act.wait_ge(qkT_done, s + 1)
                nc.scalar.activation(qT[:, :], PB[:, 0, :], ACT.Copy).then_inc(qT_ready, 1)

            def take_pT(s):
                act.wait_ge(pT_done, s + 1)
                nc.scalar.activation(pT[:, 0], PD[:, 0, :], ACT.Copy).then_inc(pT_half0, 1)

            def decay(k, n, b):
                act.wait_ge(dA_free, k + 1)
                nc.scalar.activation(dA[:, b % 2, :, 1:], dt[:, b % 2].rearrange("p (b l) -> p b l", b=B)[:, :, 1:],
                                     ACT.Exp, scale=A[:, b % 2, bass.ds(n, 1)]).then_inc(dA_ready, 1)

            def sigmoid(b):
                act.wait_ge(conv_done, b + 1)
                for i in range(DC):
                    nc.scalar.activation(y[:, i, b * L:(b + 1) * L], bank_of(b)[:, i * L:(i + 1) * L], ACT.Sigmoid,
                                         bias=cb_sb[:, i:i + 1]).then_inc(sig_ready, 1)

            def softplus_abs(b):
                act.wait_ge(dt_done, b + 1)
                for i in range(DC):
                    v = bank_of(b)[:, i * L:(i + 1) * L]
                    nc.scalar.activation(du[:, i, b * L:(b + 1) * L], v, ACT.Abs, bias=dtb_sb[:, i:i + 1])\
                        .then_inc(sp_abs, 1)
                    nc.scalar.activation(dt[:, i, b * L:(b + 1) * L], v, ACT.Relu, bias=dtb_sb[:, i:i + 1])\
                        .then_inc(sp_relu, 1)

            def softplus_exp(b):
                act.wait_ge(sp_abs, (b + 1) * DC)
                nc.scalar.activation(du[:, :, b * L:(b + 1) * L], du[:, :, b * L:(b + 1) * L], ACT.Exp, scale=-1.0)\
                    .then_inc(sp_exp, 1)

            sigmoid(0)
            sigmoid(1)
            sigmoid(2)
            softplus_abs(0)
            sigmoid(3)
            softplus_abs(1)
            nc.scalar.preload_act_table_set("natural_log_exp_and_others")
            nc.scalar.activation(expA[:, :, :], alog_sb[:, :, :], ACT.Exp).then_inc(expA_ready, 1)
            softplus_exp(0)
            softplus_exp(1)
            softplus_abs(2)
            softplus_exp(2)
            norm(0, 0)
            softplus_abs(3)
            softplus_exp(3)
            nc.scalar.preload_act_table_set("natural_log")
            act.wait_ge(sp_exp, B)
            for i in range(DC):
                nc.scalar.activation(ln_out[:, i], du[:, i], ACT.Ln, bias=1.0).then_inc(sp_ln, 1)
            nc.scalar.preload_act_table_set("natural_log_exp_and_others")
            take_qT(0)
            act.wait_ge(A_ready, 1)

            def body(g):
                for b in range(B):
                    s = g * B + b
                    if has_step(g, b, 1):
                        norm(s + 1, b + 1)
                    if has_step(g, b, -1):
                        take_pT(s - 1)
                    if has_step(g, b, 1):
                        take_qT(s + 1)
                    act.wait_ge(nbias_ready, s + 1)
                    for t in range(LT):
                        for j in range(REP):
                            k = t * REP + j
                            r = t * (REP + 1) + j
                            last = nc.scalar.activation(probs[:, b % 2, t, j], PC[:, t, j * L:(j + 1) * L], ACT.Exp,
                                                        bias=nbias[:, b % 2, k:k + 1], scale=rinv[:, b % 2, r:r + 1],
                                                        accum_out=rowsum[:, b % 2, k:k + 1])
                    last.then_inc(exp_done, 1)
                    if fixed(g) and g == 0 and b < DC:
                        act.wait_ge(dt_ready, b + 1)
                    decay(s, g * 2 + b // 2, b)

            groups(act, body)

            def take_oT(b):
                act.wait_ge(wo_done, b + 1)
                nc.scalar.activation(oT.rearrange("p c n -> p (c n)"), PA[:, 0, :], ACT.Copy).then_inc(oT_ready, 1)

            def rstd_of(k, b):
                act.wait_ge(mv_ready[k], b + 1)
                nc.scalar.activation(lnv[:, k], mv[:, k, :, 1], ACT.Ln, bias=eps_ln[:, :]).then_inc(lnv_ready[k], 1)
                act.wait_ge(lnv_ready[k], b + 1)
                nc.scalar.activation(rstd[:, k], lnv[:, k], ACT.Exp, scale=-0.5).then_inc(rstd_ready[k], 1)

            def squares(b):
                for t in range(LT):
                    act.wait_ge(relu_ready, b * LT + t + 1)
                    nc.scalar.activation(act_sq[:, t], act_sq[:, t], ACT.Square).then_inc(sq_ready, 1)

            def take_levels(b):
                for t, bank in enumerate((PA[:, 1, :], PB[:, 0, :])):
                    act.wait_ge(act_T_done, b * LT + t + 1)
                    nc.scalar.activation(act_qT[:, t].rearrange("p c n -> p (c n)"), bank.bitcast(bf16), ACT.Copy)\
                        .then_inc(act_qT_ready, 1)

            take_oT(0)

            def tail(i):
                if begins(i):
                    rstd_of(0, i)
                    nc.scalar.preload_act_table_set("sigmoid_and_others")
                    act.wait_ge(xn_ready[0], i + 1)
                    nc.scalar.activation(gate, x1, ACT.Sigmoid).then_inc(gate_ready, 1)
                    nc.scalar.preload_act_table_set("natural_log_exp_and_others")
                if fixed(i) and i == 0:
                    take_pT(STEPS - 1)
                if ends(i) and begins(i):
                    squares(i - 1)
                if begins(i):
                    rstd_of(1, i)
                    act.wait_ge(x2T_done, i + 1)
                    nc.scalar.activation(parts[:, 0], PB[:, 1, :].rearrange("p (c n) -> p c n", c=HC), ACT.Copy,
                                         scale=PART_SCALE)\
                        .then_inc(part1_ready, 1)
                if ends(i) and begins(i):
                    take_levels(i - 1)
                if final(i):
                    squares(i)
                    take_levels(i)
                if ends(i):
                    rstd_of(2, i - 1)
                if follows(i):
                    take_oT(i + 1)

            batches(act, tail)

        @block.vector
        def _(dve):
            nc.vector.memset(eps_rms[:, :], RMS_EPS).then_inc(eps_ready, 1)
            nc.vector.memset(eps_ln[:, :], LN_EPS).then_inc(eps_ready, 1)
            dve.wait_ge(ssm_in, 32)
            nc.vector.tensor_tensor(win, cw_sb, in_sb.unsqueeze(1).to_broadcast([P, TAPS, DI]), ALU.mult)\
                .then_inc(win_ready, 1)
            dve.wait_ge(xT_in, 48)
            nc.vector.scalar_tensor_tensor(wqk[:, :], qn_sb[:, :], SCALE, kn_sb[:, :], ALU.mult, ALU.mult)\
                .then_inc(wqk_ready, 1)

            def take_k(s, b):
                dve.wait_ge(rinv_ready, s + 1)
                dve.wait_ge(k_raw_ready, s + 1)
                for t in range(LT):
                    r = t * (REP + 1) + REP
                    last = nc.vector.tensor_scalar(qk_raw[:, t, REP * HD:], qk_raw[:, t, REP * HD:],
                                                   rinv[:, b % 2, r:r + 1], None, ALU.mult)
                last.then_inc(k_norm_ready, 1)

            def take_kT(s):
                dve.wait_ge(qkT_done, s + 1)
                nc.vector.tensor_scalar(kT[:, :], PB[:, 1, 0:L], wqk[:, 0:1], None, ALU.mult).then_inc(kT_ready, 1)

            def take_pT(s):
                dve.wait_ge(pT_done, s + 1)
                nc.vector.tensor_copy(pT[:, 1], PD[:, 1, :]).then_inc(pT_half1, 1)

            def take_attn(g, b, s):
                dve.wait_ge(pv_done, s + 1)
                nc.vector.tensor_copy(attnT[:, bass.ds(g * REP, REP), b * L:(b + 1) * L],
                                      PD[:, 0, :].rearrange("p (j l) -> p j l", j=REP)).then_inc(attn_ready, 1)

            def input_of(k, n, b):
                dve.wait_ge(bc_loaded[b // 2], n * 16)
                nc.vector.tensor_tensor(dBu, du[:, b % 2], bc[:, b // 2, 0], ALU.mult).then_inc(dBu_ready, 1)

            def scan(k, b):
                dve.wait_ge(dBu_ready, k + 1)
                dve.wait_ge(dA_ready, k + 1)
                nc.vector.tensor_tensor_scan(st, dA[:, b % 2].rearrange("p b l -> p (b l)"), dBu, 0.0,
                                             ALU.mult, ALU.add).then_inc(dA_free, 1)

            def output_of(k, b):
                dve.wait_ge(dA_free, k + 3)
                dve.wait_ge(y_added, k + 1)
                nc.vector.tensor_tensor(prod[:, b % 2], st, bc[:, b // 2, 1], ALU.mult).then_inc(prod_ready, 1)

            def silu(b):
                at = slice(b * L, (b + 1) * L)
                dve.wait_ge(sig_ready, (b + 1) * DC)
                for i in range(DC):
                    last = nc.vector.scalar_tensor_tensor(u[:, i, at], bank_of(b)[:, i * L:(i + 1) * L],
                                                          cb_sb[:, i:i + 1], y[:, i, at], ALU.add, ALU.mult)
                last.then_inc(u_ready, 1)

            def take_xdbl(b):
                dve.wait_ge(xdbl_done, b + 1)
                nc.vector.tensor_copy(xdbl[:, b * L:(b + 1) * L], PB[0:BC + RANK, 1, L:2 * L]).then_inc(xdbl_ready, 1)

            def softplus_rest(b):
                at = slice(b * L, (b + 1) * L)
                dve.wait_ge(sp_exp, b + 1)
                nc.vector.tensor_scalar(y[:, :, at], du[:, :, at], 1.0, -1.0, ALU.add, ALU.add).then_inc(sp_w1, 1)
                dve.wait_ge(sp_w1, b + 1)
                nc.vector.tensor_tensor(lost, du[:, :, at], y[:, :, at], ALU.subtract).then_inc(sp_lost, 1)
                dve.wait_ge(sp_lost, b + 1)
                dve.wait_ge(sp_relu, (b + 1) * DC)
                nc.vector.tensor_tensor(dt[:, :, at], dt[:, :, at], lost, ALU.add).then_inc(sp_rest, 1)

            def softplus_gate(i):
                dve.wait_ge(sp_ln, i + 1)
                dve.wait_ge(sp_w1, B)
                nc.vector.scalar_tensor_tensor(ln_out[:, i], y[:, i], 0.0, ln_out[:, i], ALU.is_gt, ALU.mult)\
                    .then_inc(sp_gate, 1)

            def softplus_end(i):
                dve.wait_ge(sp_gate, i + 1)
                dve.wait_ge(sp_rest, B)
                nc.vector.tensor_tensor(dt[:, i], dt[:, i], ln_out[:, i], ALU.add).then_inc(dt_ready, 1)
                dve.wait_ge(dt_ready, i + 1)
                nc.vector.tensor_tensor(du[:, i], dt[:, i], u[:, i], ALU.mult).then_inc(du_ready, 1)
                dve.wait_ge(du_ready, i + 1)

            def ternary(k, w, q, part):
                if part == 0:
                    dve.wait_ge((fc_in, pr_in)[k], 16)
                    nc.vector.tensor_reduce(asum[:, k:k + 1], w, AX.XY, ALU.add, apply_absolute_value=True)\
                        .then_inc(abs_ready, 1)
                elif part == 1:
                    dve.wait_ge(abs_summed, k + 1)
                    nc.vector.tensor_scalar(wscale[:, k:k + 1], atot[:, k:k + 1], 1.0 / (HID * FF), Q_EPS,
                                            ALU.mult, ALU.max).then_inc(wscale_ready, 1)
                    dve.wait_ge(wscale_ready, k + 1)
                    nc.vector.reciprocal(winv[:, k:k + 1], wscale[:, k:k + 1]).then_inc(winv_ready, 1)
                    if k == 0:
                        nc.vector.tensor_scalar(up_c[:, :], wscale[:, 0:1], wscale[:, 0:1], LEVELS,
                                                ALU.mult, ALU.mult).then_inc(up_ready, 1)
                    else:
                        nc.vector.tensor_scalar(down_c[:, :], wscale[:, 1:2], 1.0 / LEVELS, None, ALU.mult)\
                            .then_inc(up_ready, 1)
                    dve.wait_ge(winv_ready, k + 1)
                    nc.vector.tensor_scalar(w, w, winv[:, k:k + 1], ROUND, ALU.mult, ALU.add).then_inc(w_scaled, 1)
                elif part == 2:
                    dve.wait_ge(w_scaled, k + 1)
                    nc.vector.tensor_scalar(w, w, -ROUND, 1.0, ALU.add, ALU.min).then_inc(w_clipped, 1)
                else:
                    dve.wait_ge(w_clipped, k + 1)
                    dve.wait_ge(proj_done, STEPS * LT)
                    nc.vector.tensor_scalar(q, w, -1.0, (1.0 / PART_SCALE, 1.0)[k], ALU.max, ALU.mult)\
                        .then_inc(ternary_ready, 1)

            silu(0)
            silu(1)
            take_xdbl(0)
            silu(2)
            take_xdbl(1)
            silu(3)
            take_xdbl(2)
            softplus_rest(0)
            softplus_rest(1)
            take_xdbl(3)
            softplus_rest(2)
            dve.wait_ge(expA_ready, 1)
            nc.vector.tensor_scalar(A[:, :, :], expA[:, :, :], -1.0, None, ALU.mult).then_inc(A_ready, 1)
            take_k(0, 0)
            dve.wait_ge(wqk_ready, 1)
            take_kT(0)
            softplus_rest(3)
            softplus_gate(0)
            softplus_end(0)
            softplus_gate(1)

            def body(g):
                for b in range(B):
                    s = g * B + b
                    if has_step(g, b, 1):
                        take_k(s + 1, b + 1)
                    dve.wait_ge(scores_done, s + 1)
                    nc.vector.tensor_reduce(mx[:, :], PC[:, :, :].rearrange("p t (j k) -> p (t j) k", j=REP), AX.X,
                                            ALU.max).then_inc(mx_ready, 1)
                    dve.wait_ge(mx_ready, s + 1)
                    nc.vector.scalar_tensor_tensor(
                        nbias[:, b % 2].rearrange("p (t j) -> p t j", t=LT), mx[:, :].rearrange("p (t j) -> p t j", t=LT),
                        -1.0, rinv[:, b % 2].rearrange("p (t j) -> p t j", t=LT)[:, :, 0:REP], ALU.mult, ALU.mult)\
                        .then_inc(nbias_ready, 1)
                    if has_step(g, b, -1):
                        take_pT(s - 1)
                    if has_step(g, b, 1):
                        take_kT(s + 1)
                    if fixed(g) and g == 0 and b == 0:
                        softplus_end(1)
                    input_of(s, g + 1, b)
                    if fixed(g) and g == KV_HEADS - 1:
                        ternary(0, fc_sb, w1q, b)
                    dve.wait_ge(exp_done, s + 1)
                    nc.vector.reciprocal(rsinv[:, b % 2], rowsum[:, b % 2]).then_inc(rsinv_ready, 1)
                    scan(s, b)
                    if has_step(g, b, -1):
                        take_attn(*((g, b - 1) if b else (g - 1, B - 1)), s - 1)
                    output_of(s, b)

            groups(dve, body)

            def moments(k, b, src):
                for t in range(LT):
                    last = nc.vector.bn_stats(stats[:, k, t], src[:, t])
                last.then_inc(stats_ready[k], 1)
                dve.wait_ge(eps_ready, 2)
                dve.wait_ge(stats_ready[k], b + 1)
                for t in range(LT):
                    last = nc.vector.bn_aggr(mv[:, k, t], stats[:, k, t])
                last.then_inc(mv_ready[k], 1)

            def apply(k, b, src, dst):
                dve.wait_ge(rstd_ready[k], b + 1)
                for t in range(LT):
                    last = nc.vector.tensor_scalar(dst[:, t], src[:, t], mv[:, k, t, 0:1], rstd[:, k, t:t + 1],
                                                   ALU.subtract, ALU.mult)
                last.then_inc(xn_ready[k], 1)

            def relu(b, t):
                dve.wait_ge(up_done, b * LT + t + 1)
                nc.vector.tensor_scalar(act_sq[:, t], (PC, PD)[t][:, :, :].rearrange("p a n -> p (a n)"), 0.0, None,
                                        ALU.max, ALU.max, accum_out=hmax[:, t:t + 1]).then_inc(relu_ready, 1)

            def row_scales(b):
                dve.wait_ge(relu_ready, b * LT + LT)
                nc.vector.tensor_scalar(hs[:, :], hmax[:, :], wscale[:, 0:1], None, ALU.mult).then_inc(hs_ready, 1)
                dve.wait_ge(hs_ready, b + 1)
                nc.vector.tensor_tensor(hs2[:, :], hs[:, :], hs[:, :], ALU.mult).then_inc(hs2_ready, 1)
                dve.wait_ge(hs2_ready, b + 1)
                nc.vector.tensor_scalar(xmax[:, :], hs2[:, :], Q_EPS, None, ALU.max).then_inc(xmax_ready, 1)
                dve.wait_ge(xmax_ready, b + 1)
                nc.vector.reciprocal(xinv[:, :], xmax[:, :]).then_inc(xinv_ready, 1)
                nc.vector.tensor_scalar(o_mul[:, :], xmax[:, :], down_c[:, 0:1], None, ALU.mult).then_inc(mul_ready, 1)
                dve.wait_ge(xinv_ready, b + 1)
                nc.vector.tensor_scalar(q_mul[:, :], xinv[:, :], up_c[:, 0:1], None, ALU.mult).then_inc(mul_ready, 1)

            def levels(b):
                dve.wait_ge(mul_ready, b * 2 + 2)
                for t in range(LT):
                    dve.wait_ge(sq_ready, b * LT + t + 1)
                    nc.vector.tensor_scalar(act_sq[:, t], act_sq[:, t], q_mul[:, t:t + 1], ROUND, ALU.mult, ALU.add)\
                        .then_inc(rounded, 1)
                for t in range(LT):
                    dve.wait_ge(rounded, b * LT + t + 1)
                    nc.vector.tensor_scalar(act_q[:, t], act_sq[:, t], -ROUND, None, ALU.add).then_inc(act_q_ready, 1)

            def tail(i):
                if begins(i):
                    if fixed(i) and i == 0:
                        dve.wait_ge(x_in, 16)
                    dve.wait_ge(back_done, i + 1)
                    nc.vector.tensor_tensor(x1p, PA[:, 1, :].rearrange("p (t n) -> p t n", t=LT),
                                            x_sb[:, bass.ds(i * LT, LT)], ALU.add).then_inc(xp_ready[0], 1)
                    dve.wait_ge(xp_ready[0], i + 1)
                    moments(0, i, x1p)
                    apply(0, i, x1p, x1)
                if fixed(i) and i == 0:
                    take_pT(STEPS - 1)
                if ends(i) and begins(i):
                    relu(i - 1, 0)
                if begins(i):
                    dve.wait_ge(gate_ready, i + 1)
                    nc.vector.tensor_tensor(gate, gate, x1, ALU.mult).then_inc(z_ready, 1)
                    if fixed(i) and i == 0:
                        for part in range(2):
                            ternary(1, pr_sb, w2q, part)
                        take_attn(KV_HEADS - 1, B - 1, STEPS - 1)
                        dve.wait_ge(y_added, STEPS + DC)
                    dve.wait_ge(z_ready, i + 1)
                    nc.vector.tensor_tensor(gated, gate, y[:, :, bass.ds(i * L, L)], ALU.mult).then_inc(gated_ready, 1)
                if ends(i) and begins(i):
                    relu(i - 1, 1)
                if begins(i):
                    dve.wait_ge(gT_done, i + 1)
                    nc.vector.tensor_tensor(x2p, PB[:, 0, :].rearrange("p (t n) -> p t n", t=LT), x1, ALU.add)\
                        .then_inc(xp_ready[1], 1)
                    dve.wait_ge(xp_ready[1], i + 1)
                    moments(1, i, x2p)
                if ends(i) and begins(i):
                    row_scales(i - 1)
                if begins(i):
                    apply(1, i, x2p, x2)
                if ends(i) and begins(i):
                    levels(i - 1)
                if begins(i):
                    dve.wait_ge(part1_ready, i + 1)
                    nc.vector.scalar_tensor_tensor(parts[:, 1], PB[:, 1, :].rearrange("p (c n) -> p c n", c=HC),
                                                   PART_SCALE, parts[:, 0], ALU.mult, ALU.subtract)\
                        .then_inc(part2_ready, 1)
                if fixed(i) and i == 0:
                    for part in range(2, 4):
                        ternary(1, pr_sb, w2q, part)
                if final(i):
                    for t in range(LT):
                        relu(i, t)
                if ends(i):
                    if not begins(i):
                        dve.wait_ge(xn_ready[2], i - 1)
                    dve.wait_ge(down_done, i * LT)
                    for t in range(LT):
                        last = nc.vector.scalar_tensor_tensor(x3p[:, t], PB[:, 1, t * HID:(t + 1) * HID],
                                                              o_mul[:, t:t + 1], x2_kept[:, t], ALU.mult, ALU.add)
                    last.then_inc(xp_ready[2], 1)
                    dve.wait_ge(xp_ready[2], i)
                if begins(i):
                    dve.wait_ge(xn_ready[1], i + 1)
                    nc.vector.tensor_copy(x2_kept, x2).then_inc(kept, 1)
                if final(i):
                    row_scales(i)
                    levels(i)
                if ends(i):
                    if not fixed(i) or i > 1:
                        reach(dve, stored, i * 16 - 16)
                    moments(2, i - 1, x3p)
                    apply(2, i - 1, x3p, x3)
                if begins(i):
                    dve.wait_ge(kept, i + 1)

            batches(dve, tail)

        @block.tensor
        def _(pe):
            def project_tile(g, b, t):
                for c in range(HC):
                    last = nc.tensor.matmul(PA[:, t, :], xT_sb[:, c, b * L + t * P:b * L + (t + 1) * P],
                                            w_sb[:, bass.ds(g, 1), c].rearrange("p o n -> p (o n)"),
                                            start=(c == 0), stop=(c == HC - 1))
                last.then_inc(proj_done, 1)

            def transpose_qk(s):
                pe.wait_ge(q_raw_ready, s + 1)
                pe.wait_ge(k_norm_ready, s + 1)
                for j in range(REP + 1):
                    dst = PB[:, 0, j * L:(j + 1) * L] if j < REP else PB[:, 1, 0:L]
                    for t in range(LT):
                        last = nc.tensor.transpose(dst[:, t * P:(t + 1) * P], qk_raw[:, t, j * HD:(j + 1) * HD],
                                                   ident[:, :])
                last.then_inc(qkT_done, 1)

            def scores(s):
                pe.wait_ge(qT_ready, s + 1)
                pe.wait_ge(kT_ready, s + 1)
                reach(pe, exp_done, s)
                for t in range(LT):
                    for j in range(REP):
                        windowed = t * P >= L - WINDOW
                        last = nc.tensor.matmul(PC[:, t, j * L:(j + 1) * L], qT[:, j * L + t * P:j * L + (t + 1) * P],
                                                kT[:, :], start=True, stop=not windowed)
                        if windowed:
                            last = nc.tensor.matmul(PC[:, t, j * L + P:(j + 1) * L], ident16[:, :], mask16[:, :],
                                                    start=False, stop=True)
                last.then_inc(scores_done, 1)

            def transpose_probs(s, b):
                pe.wait_ge(normed, s + 1)
                reach(pe, attn_ready, s)
                for c in range(LT):
                    for j in range(REP):
                        for t in range(LT):
                            last = nc.tensor.transpose(PD[:, c, j * L + t * P:j * L + (t + 1) * P],
                                                       probs[:, b % 2, t, j, c * P:(c + 1) * P], ident[:, :])
                last.then_inc(pT_done, 1)

            def attend(s, b):
                pe.wait_ge(pT_half0, s + 1)
                pe.wait_ge(pT_half1, s + 1)
                for c in range(LT):
                    last = nc.tensor.matmul(PD[:, 0, :], v_sb[:, b % 4, c], pT[:, c], start=(c == 0), stop=(c == LT - 1))
                last.then_inc(pv_done, 1)

            def convolve(b):
                if b == 0:
                    pe.wait_ge(win_ready, 1)
                    pe.wait_ge(ctx_in, 16)
                    pe.wait_ge(zeroed, 4)
                for i in range(DC):
                    for k in range(TAPS):
                        last = nc.tensor.matmul(bank_of(b)[:, i * L:(i + 1) * L], win[:, k, i * P:(i + 1) * P],
                                                ctxp[:, b, k:k + L], start=(k == 0), stop=(k == TAPS - 1))
                last.then_inc(conv_done, 1)

            def x_proj(b):
                pe.wait_ge(small_in, 16 * 6)
                pe.wait_ge(u_ready, b + 1)
                reach(pe, xdbl_ready, b)
                for i in range(DC):
                    last = nc.tensor.matmul(PB[0:BC + RANK, 1, L:2 * L], xp_sb[:, i], u[:, i, b * L:(b + 1) * L],
                                            start=(i == 0), stop=(i == DC - 1))
                last.then_inc(xdbl_done, 1)

            def dt_proj(b):
                pe.wait_ge(xdbl_ready, b + 1)
                for i in range(DC):
                    last = nc.tensor.matmul(bank_of(b)[:, i * L:(i + 1) * L], dtw_sb[BC:, i * P:(i + 1) * P],
                                            xdbl[BC:, b * L:(b + 1) * L], start=True, stop=True)
                last.then_inc(dt_done, 1)

            def out_project(b, first, end):
                if first == 0:
                    pe.wait_ge(attn_ready, b + (STEPS - B + 1))
                n = HC * HEADS // 8
                for k in range(first * n, end * n):
                    c, h = k // HEADS, k % HEADS
                    last = nc.tensor.matmul(PA[:, 0, c * L:(c + 1) * L], wo_sb[:, h, c * P:(c + 1) * P],
                                            attnT[:, h, bass.ds(b * L, L)], start=(h == 0), stop=(h == HEADS - 1))
                if end == 8:
                    last.then_inc(wo_done, 1)

            convolve(0)
            convolve(1)
            x_proj(0)
            convolve(2)
            dt_proj(0)
            x_proj(1)
            convolve(3)
            dt_proj(1)
            x_proj(2)
            pe.wait_ge(xT_in, 48)
            pe.wait_ge(w_in[0], 16)
            project_tile(0, 0, 0)
            dt_proj(2)
            x_proj(3)
            project_tile(0, 0, 1)
            dt_proj(3)
            pe.wait_ge(const_ready, 3)
            pe.wait_ge(xdbl_ready, B)
            transpose_qk(0)
            pe.wait_ge(v_ready, 1)
            for t in range(LT):
                project_tile(0, 1, t)
            pe.wait_ge(sp_abs, B * DC)
            pe.wait_ge(sp_relu, B * DC)

            def body(g):
                for b in range(B):
                    s = g * B + b
                    scores(s)
                    if has_step(g, b, -1):
                        transpose_probs(s - 1, b + 1)
                    if has_step(g, b, 1):
                        transpose_qk(s + 1)
                    ahead_g, ahead_b = (g, b + 2) if b + 2 < B else (g + 1, b + 2 - B)
                    if has_step(g, b, 2):
                        if b + 2 == B:
                            if fixed(g) and g == 0:
                                pe.wait_ge(w_in[1], 16)
                            else:
                                pe.wait_ge(w_rest, g * 16)
                        pe.wait_ge(v_ready, s + 2)
                        project_tile(ahead_g, ahead_b, 0)
                    elif b == 2:
                        pe.wait_ge(v_ready, STEPS)
                        pe.wait_ge(wo_in, 16)
                        out_project(0, 0, 2)
                    else:
                        out_project(0, 4, 6)
                    if has_step(g, b, -1):
                        attend(s - 1, b + 3)
                    if has_step(g, b, 2):
                        project_tile(ahead_g, ahead_b, 1)
                    elif b == 2:
                        out_project(0, 2, 4)
                    else:
                        out_project(0, 6, 8)

            groups(pe, body)

            def up(i, t):
                if t == 0:
                    pe.wait_ge(attn_ready, STEPS)
                    pe.wait_ge(ternary_ready, 1)
                    pe.wait_ge(part2_ready, i + 1)
                for half in range(2):
                    for k in range(2 * HC):
                        last = nc.tensor.matmul((PC, PD)[t][:, half, :], parts[:, k // HC, k % HC, t * P:(t + 1) * P],
                                                w1q[:, k % HC, half * 512:(half + 1) * 512],
                                                start=(k == 0), stop=(k == 2 * HC - 1))
                last.then_inc(up_done, 1)

            def tail(i):
                if ends(i) and follows(i):
                    up(i - 1, 0)
                if begins(i):
                    pe.wait_ge(oT_ready, i + 1)
                    for t in range(LT):
                        for c in range(HC):
                            last = nc.tensor.transpose(PA[:, 1, t * HID + c * P:t * HID + (c + 1) * P],
                                                       oT[:, c, t * P:(t + 1) * P], ident[:, :])
                    last.then_inc(back_done, 1)
                if final(i):
                    up(i - 1, 0)
                if ends(i) and begins(i):
                    up(i - 1, 1)
                if follows(i):
                    out_project(i + 1, 0, 2 if fixed(i) and i == 0 else 3)
                if fixed(i) and i == 0:
                    transpose_probs(STEPS - 1, B - 1)
                    out_project(i + 1, 2, 4)
                    attend(STEPS - 1, B - 1)
                    out_project(i + 1, 4, 5)
                if begins(i):
                    pe.wait_ge(gated_ready, i + 1)
                    for t in range(LT):
                        for c in range(DC):
                            last = nc.tensor.transpose(PB[:, 0, t * DI + c * P:t * DI + (c + 1) * P],
                                                       gated[:, c, t * P:(t + 1) * P], ident[:, :])
                    last.then_inc(gT_done, 1)
                if fixed(i) and i == 0:
                    out_project(i + 1, 5, 7)
                elif follows(i):
                    out_project(i + 1, 3, 5)
                if begins(i):
                    pe.wait_ge(xn_ready[1], i + 1)
                    for c in range(HC):
                        for t in range(LT):
                            last = nc.tensor.transpose(PB[:, 1, c * L + t * P:c * L + (t + 1) * P],
                                                       x2[:, t, c * P:(c + 1) * P], ident[:, :])
                    last.then_inc(x2T_done, 1)
                if follows(i) and not (fixed(i) and i == 0):
                    out_project(i + 1, 5, 6)
                if ends(i):
                    for t, bank in enumerate((PA[:, 1, :], PB[:, 0, :])):
                        pe.wait_ge(act_q_ready, i * LT - LT + t + 1)
                        for c in range(FC):
                            last = nc.tensor.transpose(bank.bitcast(bf16)[:, c * P:(c + 1) * P],
                                                       act_q[:, t, c * P:(c + 1) * P], ident16[:, :])
                        last.then_inc(act_T_done, 1)
                if follows(i) and not (fixed(i) and i == 0):
                    out_project(i + 1, 6, 7)
                if final(i):
                    for t in range(LT):
                        up(i, t)
                if ends(i):
                    pe.wait_ge(ternary_ready, 2)
                    if begins(i):
                        pe.wait_ge(part2_ready, i + 1)
                    for t in range(LT):
                        pe.wait_ge(act_qT_ready, i * LT - LT + t + 1)
                        for c in range(FC):
                            last = nc.tensor.matmul(PB[:, 1, t * HID:(t + 1) * HID], act_qT[:, t, c], w2q[:, c],
                                                    start=(c == 0), stop=(c == FC - 1))
                        last.then_inc(down_done, 1)
                if follows(i):
                    out_project(i + 1, 7, 8)

            batches(pe, tail)


def kernel(**inputs):
    import numpy as np
    import concourse.bacc as bacc
    from concourse.bass_utils import run_bass_kernel_spmd

    def columns(a, rows, cols):
        return a.reshape(rows, cols).T

    a = {k: np.asarray(v) for k, v in inputs.items()}
    x = a["x"].reshape(T, HID)
    wq = a["L0_attn_Wq"].reshape(KV_HEADS, REP * HD, HID)
    wk = a["L0_attn_Wk"].reshape(KV_HEADS, HD, HID)
    wv = a["L0_attn_Wv"].reshape(KV_HEADS, HD, HID)
    xp = a["L0_xattn_x_proj_w"]
    b_rows, c_rows = xp[RANK:RANK + NS], xp[RANK + NS:]
    bc_rows = np.stack([b_rows, c_rows], axis=1).reshape(BC, DI)
    named = {
        "x": x,
        "xT": x.T,
        "ctxT": a["ctx_1024"].reshape(T, CTX).T,
        "w_qkvT": np.concatenate([wq, wk, wv], axis=1).transpose(0, 2, 1),
        "w_oT": a["L0_attn_Wo"].T,
        "q_norm": a["L0_attn_q_norm_w"].reshape(HD, 1),
        "k_norm": a["L0_attn_k_norm_w"].reshape(HD, 1),
        "in_projT": a["L0_xattn_in_proj_w"].T,
        "conv_wT": a["L0_xattn_conv_w"].reshape(DI, TAPS).T,
        "conv_b": columns(a["L0_xattn_conv_b"], DC, P),
        "x_projT": np.concatenate([bc_rows, xp[:RANK]], axis=0).T,
        "dt_projT": a["L0_xattn_dt_proj_w"].T,
        "dt_b": columns(a["L0_xattn_dt_proj_b"], DC, P),
        "a_log": a["L0_xattn_A_log"],
        "d_skip": columns(a["L0_xattn_D"], DC, P),
        "c_fc": a["L0_ffn_c_fc"],
        "c_projT": a["L0_ffn_c_proj"].T,
    }
    nc = bacc.Bacc("TRN2", target_bir_lowering=False, num_devices=1)
    arrays, args = {}, []
    for name, v in named.items():
        v = np.ascontiguousarray(v)
        arrays[f"in_{name}"] = v
        args.append(nc.dram_tensor(f"in_{name}", v.shape, mybir.dt.from_np(v.dtype), kind="ExternalInput").ap())
    args.append(nc.dram_tensor("layer_out", (T, HID), mybir.dt.float32, kind="ExternalOutput").ap())
    decoder_layer(nc, *args)
    r = run_bass_kernel_spmd(nc, [arrays], core_ids=[0])
    return r.results[0]["layer_out"].reshape(B, L, HID)
```
